# Optimizing a Trainium2 kernel written in Bass

```python
import numpy as np
import jax
import jax.numpy as jnp

def _softmax(x, axis=-1):
    return jax.nn.softmax(x, axis=axis)

def _gelu(x):
    return jax.nn.gelu(x, approximate=True)

def _silu(x):
    return jax.nn.silu(x)

def _sigmoid(x):
    return jax.nn.sigmoid(x)

def _layernorm(x, axis=-1, eps=1e-05):
    m = jnp.mean(x, axis=axis, keepdims=True)
    v = jnp.var(x, axis=axis, keepdims=True)
    return (x - m) / jnp.sqrt(v + eps)

def _scatter_add(tgt, idx, src, axis=0):
    return tgt.at[idx].add(src)

def _segment_sum(src, seg, n):
    return jax.ops.segment_sum(src, seg, n)
kernel_name = 'mk_vit_tower_d1_tok_img512_r4_bef040'

def setup_inputs(seed: int=0):
    np.random.seed(seed)
    _w = jnp.asarray

    def _rec_inputs():
        import jax
        import jax.numpy as jnp
        _rk = jax.random.key(seed)
        x = -0.000147625 + 0.999875 * jax.random.normal(jax.random.fold_in(_rk, 1), (128, 3, 224, 224), jnp.float32)
        return x
    x = _rec_inputs()

    def _L0_tok_setup():
        import jax, jax.numpy as jnp
        import numpy as np
        N_PATCHES = 8
        PATCH = 28
        C = 3
        IN_D = C * PATCH * PATCH
        HID = 128
        SEQ = N_PATCHES * N_PATCHES + 1

        def _positional_embedding(seq_len, dim):
            i = np.arange(seq_len)[:, None].astype(np.float32)
            j = np.arange(dim)[None, :].astype(np.float32)
            ang = i / np.power(100000.0, j / dim)
            pe = np.where(j % 2 == 0, np.sin(ang), np.cos(ang))
            return jnp.asarray(pe, dtype=jnp.float32)
        key = jax.random.key(seed)
        k1, k2, k3, k4 = jax.random.split(key, 4)
        B = 64
        X = jax.random.normal(k1, (B, C, 224, 224), dtype=jnp.float32)
        bound = 1.0 / np.sqrt(IN_D)
        W = jax.random.uniform(k2, (HID, IN_D), minval=-bound, maxval=bound, dtype=jnp.float32)
        b = jax.random.uniform(k3, (HID,), minval=-bound, maxval=bound, dtype=jnp.float32)
        class_token = jax.random.uniform(k4, (1, HID), dtype=jnp.float32)
        pos_embed = _positional_embedding(SEQ, HID)
        return {'X': X, 'W': W, 'b': b, 'class_token': class_token, 'pos_embed': pos_embed}
    _L0_tok_all = _L0_tok_setup()
    _L0_tok_in = {k: v for k, v in _L0_tok_all.items() if k in ('W', 'b', 'class_token', 'pos_embed')}
    del _L0_tok_all

    def _L0_attn_setup():
        import jax, jax.numpy as jnp
        import numpy as np
        DIM = 128
        B, T = (32, 512)

        def _lstm(x, W_ih, W_hh, b_ih, b_hh):
            Bb, Tt, D = x.shape
            xg = jnp.einsum('btd,gd->btg', x, W_ih) + b_ih + b_hh
            xg = jnp.swapaxes(xg, 0, 1)

            def step(carry, xt):
                h, c = carry
                gates = xt + h @ W_hh.T
                i, f, g, o = jnp.split(gates, 4, axis=-1)
                i = jax.nn.sigmoid(i)
                f = jax.nn.sigmoid(f)
                g = jnp.tanh(g)
                o = jax.nn.sigmoid(o)
                c = f * c + i * g
                h = o * jnp.tanh(c)
                return ((h, c), h)
            h0 = jnp.zeros((Bb, D), dtype=x.dtype)
            (_, _), hs = jax.lax.scan(step, (h0, h0), xg)
            return jnp.swapaxes(hs, 0, 1)
        key = jax.random.key(seed)
        k_x, k_wih, k_whh, k_bih, k_bhh = jax.random.split(key, 5)
        s = 1.0 / np.sqrt(DIM)
        return {'x': jax.random.normal(k_x, (B, T, DIM), dtype=jnp.float32), 'W_ih': jax.random.uniform(k_wih, (4 * DIM, DIM), minval=-s, maxval=s, dtype=jnp.float32), 'W_hh': jax.random.uniform(k_whh, (4 * DIM, DIM), minval=-s, maxval=s, dtype=jnp.float32), 'b_ih': jax.random.uniform(k_bih, (4 * DIM,), minval=-s, maxval=s, dtype=jnp.float32), 'b_hh': jax.random.uniform(k_bhh, (4 * DIM,), minval=-s, maxval=s, dtype=jnp.float32)}
    _L0_attn_all = _L0_attn_setup()
    _L0_attn_in = {k: v for k, v in _L0_attn_all.items() if k in ('W_ih', 'W_hh', 'b_ih', 'b_hh')}
    del _L0_attn_all

    def _L0_ffn_setup():
        import jax, jax.numpy as jnp
        import numpy as np
        from jax import lax
        N_EXPERTS = 16
        TOP_K = 2
        D_MODEL = 128
        D_FF = 512
        key = jax.random.key(seed)
        ks = jax.random.split(key, 7)
        s_in = 1.0 / np.sqrt(D_MODEL)
        s_ff = 1.0 / np.sqrt(D_FF)
        x = jax.random.normal(ks[0], (2, 512, D_MODEL), dtype=jnp.float32)
        router_w = jax.random.uniform(ks[1], (N_EXPERTS, D_MODEL), jnp.float32, -s_in, s_in)
        router_b = jax.random.uniform(ks[2], (N_EXPERTS,), jnp.float32, -s_in, s_in)
        w1 = jax.random.uniform(ks[3], (N_EXPERTS, D_FF, D_MODEL), jnp.float32, -s_in, s_in)
        b1 = jax.random.uniform(ks[4], (N_EXPERTS, D_FF), jnp.float32, -s_in, s_in)
        w2 = jax.random.uniform(ks[5], (N_EXPERTS, D_MODEL, D_FF), jnp.float32, -s_ff, s_ff)
        b2 = jax.random.uniform(ks[6], (N_EXPERTS, D_MODEL), jnp.float32, -s_ff, s_ff)
        return {'x': x, 'router_w': router_w, 'router_b': router_b, 'w1': w1, 'b1': b1, 'w2': w2, 'b2': b2}
    _L0_ffn_all = _L0_ffn_setup()
    _L0_ffn_in = {k: v for k, v in _L0_ffn_all.items() if k in ('router_w', 'router_b', 'w1', 'b1', 'w2', 'b2')}
    del _L0_ffn_all
    return {'x': x, 'L0_tok_W': _L0_tok_in['W'], 'L0_tok_b': _L0_tok_in['b'], 'L0_tok_class_token': _L0_tok_in['class_token'], 'L0_tok_pos_embed': _L0_tok_in['pos_embed'], 'L0_attn_W_ih': _L0_attn_in['W_ih'], 'L0_attn_W_hh': _L0_attn_in['W_hh'], 'L0_attn_b_ih': _L0_attn_in['b_ih'], 'L0_attn_b_hh': _L0_attn_in['b_hh'], 'L0_ffn_router_w': _L0_ffn_in['router_w'], 'L0_ffn_router_b': _L0_ffn_in['router_b'], 'L0_ffn_w1': _L0_ffn_in['w1'], 'L0_ffn_b1': _L0_ffn_in['b1'], 'L0_ffn_w2': _L0_ffn_in['w2'], 'L0_ffn_b2': _L0_ffn_in['b2']}

def reference(x, L0_tok_W, L0_tok_b, L0_tok_class_token, L0_tok_pos_embed, L0_attn_W_ih, L0_attn_W_hh, L0_attn_b_ih, L0_attn_b_hh, L0_ffn_router_w, L0_ffn_router_b, L0_ffn_w1, L0_ffn_b1, L0_ffn_w2, L0_ffn_b2):
    import jax
    import jax.numpy as jnp

    def _L0_tok_ref(X, W, b, class_token, pos_embed):
        import jax, jax.numpy as jnp
        import numpy as np
        N_PATCHES = 8
        PATCH = 28
        C = 3
        IN_D = C * PATCH * PATCH
        HID = 128
        SEQ = N_PATCHES * N_PATCHES + 1

        def _positional_embedding(seq_len, dim):
            i = np.arange(seq_len)[:, None].astype(np.float32)
            j = np.arange(dim)[None, :].astype(np.float32)
            ang = i / np.power(100000.0, j / dim)
            pe = np.where(j % 2 == 0, np.sin(ang), np.cos(ang))
            return jnp.asarray(pe, dtype=jnp.float32)
        B = X.shape[0]
        patches = X.reshape(B, C, N_PATCHES, PATCH, N_PATCHES, PATCH)
        patches = patches.transpose(0, 2, 4, 1, 3, 5).reshape(B, N_PATCHES * N_PATCHES, IN_D)
        tokens = jnp.einsum('bpi,hi->bph', patches, W) + b
        cls = jnp.broadcast_to(class_token[None, :, :], (B, 1, HID))
        tokens = jnp.concatenate([cls, tokens], axis=1)
        return tokens * pos_embed[None, :, :]

    def _L0_attn_ref(x, W_ih, W_hh, b_ih, b_hh):
        import jax, jax.numpy as jnp
        import numpy as np
        DIM = 128
        B, T = (32, 512)

        def _lstm(x, W_ih, W_hh, b_ih, b_hh):
            Bb, Tt, D = x.shape
            xg = jnp.einsum('btd,gd->btg', x, W_ih) + b_ih + b_hh
            xg = jnp.swapaxes(xg, 0, 1)

            def step(carry, xt):
                h, c = carry
                gates = xt + h @ W_hh.T
                i, f, g, o = jnp.split(gates, 4, axis=-1)
                i = jax.nn.sigmoid(i)
                f = jax.nn.sigmoid(f)
                g = jnp.tanh(g)
                o = jax.nn.sigmoid(o)
                c = f * c + i * g
                h = o * jnp.tanh(c)
                return ((h, c), h)
            h0 = jnp.zeros((Bb, D), dtype=x.dtype)
            (_, _), hs = jax.lax.scan(step, (h0, h0), xg)
            return jnp.swapaxes(hs, 0, 1)
        return _lstm(x, W_ih, W_hh, b_ih, b_hh)

    def _L0_ffn_ref(x, router_w, router_b, w1, b1, w2, b2):
        import jax, jax.numpy as jnp
        import numpy as np
        from jax import lax
        N_EXPERTS = 16
        TOP_K = 2
        D_MODEL = 128
        D_FF = 512
        B, S, D = x.shape
        xt = x.reshape(-1, D)
        logits = xt @ router_w.T + router_b
        probs = jax.nn.softmax(logits, axis=-1)
        topk_p, topk_i = lax.top_k(probs, TOP_K)
        onehot = jax.nn.one_hot(topk_i, N_EXPERTS, dtype=probs.dtype)
        gates = jnp.sum(onehot * topk_p[..., None], axis=1)

        def expert_step(acc, packed):
            w1e, b1e, w2e, b2e, ge = packed
            h = jax.nn.gelu(xt @ w1e.T + b1e, approximate=False)
            y = h @ w2e.T + b2e
            return (acc + y * ge[:, None], None)
        out, _ = lax.scan(expert_step, jnp.zeros_like(xt), (w1, b1, w2, b2, gates.T))
        return out.reshape(B, S, D)
    h = _L0_tok_ref(x, L0_tok_W, L0_tok_b, L0_tok_class_token, L0_tok_pos_embed)
    h = h + _L0_attn_ref(_layernorm(h, axis=-1), L0_attn_W_ih, L0_attn_W_hh, L0_attn_b_ih, L0_attn_b_hh)
    h = h + _L0_ffn_ref(_layernorm(h, axis=-1), L0_ffn_router_w, L0_ffn_router_b, L0_ffn_w1, L0_ffn_b1, L0_ffn_w2, L0_ffn_b2)
    return h

_drawn_inputs = setup_inputs


def setup_inputs(seed=0):
    import zlib

    import numpy as np

    out = dict(_drawn_inputs(seed))
    spreads = {}
    factors = {'L0_ffn_b1': 6.86, 'L0_ffn_b2': 4.748}
    for name, (base, spread) in spreads.items():
        noise = np.random.default_rng([zlib.crc32(name.encode()), seed]).standard_normal(out[name].shape)
        drawn = base * np.exp(spread * noise) if base else spread * noise
        out[name] = jnp.asarray(drawn.astype(out[name].dtype))
    for name, factor in factors.items():
        out[name] = (out[name] * factor).astype(out[name].dtype)
    return out
```

```python
from contextlib import ExitStack

import numpy as np

import concourse.bass as bass
from concourse import mybir

P = 128
B, C, IMG, GRID, HID = 128, 3, 224, 8, 128
PATCH = IMG // GRID
IN_D = C * PATCH * PATCH
T = GRID * GRID + 1
KC = IN_D // P
KREST = IN_D - KC * P
E, FF = 16, 512
FC = FF // P
TOKENS = T * B
CAP = TOKENS + P
TILES_B = (2 * TOKENS - E) // P + E
ROW = HID + 2
EPS = 1e-5
W_SCALE = 1024.0
E_SCALE = 256.0
PIECE = 256
PIECES = E * 2 * FF // PIECE
U = 8
UB = 4
NX = 4
NP_ = 4
NY = 8
NO_TOKEN = 1 << 20
CT = 5
NC_ = 3

C_ID, C_TRI, C_ONE, C_IOTA, C_EBASE, C_TOK, C_BSC, C_POW, C_J = np.cumsum([0, P, P, P, U * E, E, T, 4, 1]).tolist()
C_END = C_J + TILES_B


def constants():
    c = np.zeros((P, C_END), np.float32)
    c[:, C_ID:C_TRI] = np.eye(P)
    c[:, C_TRI:C_ONE] = np.triu(np.ones((P, P)), 1)
    c[:, C_ONE:C_IOTA] = 1.0
    c[:, C_IOTA:C_EBASE] = np.tile(np.arange(E), U)
    c[:, C_EBASE:C_TOK] = np.arange(E) * CAP
    c[:, C_TOK:C_BSC] = np.arange(P)[:, None] + P * np.arange(T)
    c[:, C_POW] = -0.5
    c[:, C_BSC:C_POW] = [0.5, 0.5, 1.0, 0.5]
    c[:, C_J:] = P * np.arange(TILES_B)
    return c


class At:

    def __init__(self, reg, at, width):
        self.reg, self.at, self.width = reg, at, width

    def __add__(self, k):
        return At(self.reg, self.at + k, self.width)

    def __sub__(self, k):
        return self + -k

    def within(self, low, high):
        return self.reg is not None or low <= self.at <= high

    def val(self):
        return self.at if self.reg is None else self.reg * self.width + self.at

    def mod(self, m):
        assert self.width % m == 0 or self.reg is None
        return self.at % m

    def div(self, m):
        assert self.width % m == 0 or self.reg is None
        return self.at // m if self.reg is None else self.reg * (self.width // m) + self.at // m


def tower(nc, x, w, w_rest, bias, cls, pos, w_ih, w_hh, b_ih, b_hh, rw, rb, we, b1, b2, const, out):
    F32, F16, I32, U32 = mybir.dt.float32, mybir.dt.float16, mybir.dt.int32, mybir.dt.uint32
    ALU, ACT, AX = mybir.AluOpType, mybir.ActivationFunctionType, mybir.AxisListType
    ctx = ExitStack()
    with ctx:
        def sb(name, shape, dt=F32):
            return ctx.enter_context(nc.sbuf_tensor(name, shape, dt))

        def sem(name):
            return ctx.enter_context(nc.semaphore(name))

        sent = nc.dram_tensor("sent", [E * CAP + P, ROW], F32, kind="Internal").ap()
        back = nc.dram_tensor("back", [2 * TOKENS, HID], F32, kind="Internal").ap()

        cst = sb("cst", [P, C_END])
        ident16 = sb("ident16", [P, P], F16)
        tri16 = sb("tri16", [P, P], F16)
        ones16 = sb("ones16", [P, P], F16)
        xraw = [sb(f"xraw{i}", [P, KC + 1, P]) for i in range(NX)]
        xhi = [sb(f"xhi{i}", [P, KC + 1, P], F16) for i in range(2)]
        xlo = [sb(f"xlo{i}", [P, KC + 1, P], F16) for i in range(2)]
        whi = sb("whi", [P, KC + 1, HID], F16)
        wlo = sb("wlo", [P, KC + 1, HID], F16)
        biasw = sb("biasw", [P, HID])
        posr = sb("posr", [P, NP_, HID])
        wih = sb("wih", [HID, 4, HID])
        whh = sb("whh", [HID, 4, HID])
        lbias = sb("lbias", [HID, 3, 4])
        rws = sb("rws", [HID, E])
        rbs = sb("rbs", [P, U, E])
        ex_hi = sb("ex_hi", [P, E, 2, FF], F16)
        ex_lo = sb("ex_lo", [P, E, 2, FF], F16)
        ex_raw = sb("ex_raw", [P, 4, PIECE])
        b1s = sb("b1s", [P, E * FC])
        b2r = sb("b2r", [P, 4, HID])
        h0 = sb("h0", [P, 4, HID])
        tok_sum = sb("tok_sum", [P, HID])
        stats = sb("stats", [P, 2, 6])
        mv = sb("mv", [P, 2, 2])
        veps = sb("veps", [P, 2])
        rstd = sb("rstd", [P, 2])
        xn = sb("xn", [P, 2, HID])
        xnT = sb("xnT", [HID, 2, B])
        gate = sb("gate", [HID, 4, B])
        c2 = sb("c2", [HID, B])
        ca = sb("ca", [HID, B])
        cb = sb("cb", [HID, B])
        tc = sb("tc", [HID, B])
        h2 = sb("h2", [HID, 2, B])
        h1 = sb("h1", [P, T, HID])
        yn = sb("yn", [P, NY, HID])
        ynT = sb("ynT", [HID, 2, B])
        pay = sb("pay", [P, NY, ROW])
        lg = sb("lg", [P, U, E])
        pr = sb("pr", [P, U, E])
        pr2 = sb("pr2", [P, U, E])
        cand = sb("cand", [P, U, E])
        oh = sb("oh", [P, 2, U, E])
        mask16 = sb("mask16", [P, U, E], F16)
        rank = sb("rank", [P, U, E])
        red = sb("red", [P, 8, U])
        gates = sb("gates", [P, 2, T])
        first = sb("first", [P, T])
        count = sb("count", [P, E])
        slotf = sb("slotf", [P, 2, U])
        slot = sb("slot", [P, 2, U], I32)
        slot_own = sb("slot_own", [P, 2, U], I32)
        tabs = sb("tabs", [P, 12, E])
        tabi = sb("tabi", [1, 2, TILES_B], I32)
        padi = sb("padi", [1, E], I32)
        pad = sb("pad", [P, ROW])

        def flat(t):
            return t[:, :, :].rearrange("p a b -> p (a b)")

        xt = [flat(xraw[0])[:, i * ROW:(i + 1) * ROW] for i in range(4)]
        hf = [flat(xraw[0])[:, 1024 + i * FF:1024 + (i + 1) * FF] for i in range(2)]
        xTs = [flat(xraw[1])[:, i * P:(i + 1) * P].bitcast(F16) for i in range(2)]
        hhi = [flat(xraw[1])[:, 512 + i * FF // 2:512 + (i + 1) * FF // 2].bitcast(F16) for i in range(2)]
        hlo = [flat(xraw[1])[:, 1024 + i * FF // 2:1024 + (i + 1) * FF // 2].bitcast(F16) for i in range(2)]
        yo = [flat(xraw[2])[:, i * HID:(i + 1) * HID] for i in range(4)]
        dsto = [flat(xraw[2])[:, 1024 + i:1025 + i].bitcast(I32) for i in range(4)]
        dsti = [flat(xraw[2])[:, 1032 + i:1033 + i].bitcast(I32) for i in range(4)]
        big = flat(xraw[1])[:, 0:TILES_B * E]
        big2 = flat(xraw[2])[:, 0:TILES_B * E]
        tabj = flat(xraw[3])[:, 0:4 * TILES_B].rearrange("p (a j) -> p a j", a=4)
        bk = [xraw[i][:, 0:2 * CT, :] for i in range(NC_)]

        bank = [ctx.enter_context(nc.psum_tensor(f"bank{i}", [P, 512], F32)) for i in range(8)]
        ps_tok = bank[0:2]
        ps_gate = bank[2:4]
        ps_T, ps_h, ps_logit, ps_rank = bank[4:8]
        ps_up = bank[2:4]
        ps_down = bank[0:2]
        ps_in = [b[:, 0:P].bitcast(F16) for b in bank[4:6]]

        const_in = sem("const_in")
        w_in = sem("w_in")
        setup_act = sem("setup_act")
        setup_dve = sem("setup_dve")
        setup_pool = sem("setup_pool")
        x_in = [sem(f"x_in{i}") for i in range(NX)]
        pos_in = [sem(f"pos_in{i}") for i in range(NP_)]
        hi_done, lo_done, tok_done = sem("hi_done"), sem("lo_done"), sem("tok_done")
        biased, h0_done = sem("biased"), sem("h0_done")
        st1, mv1, ve1, rs1, xn_done = sem("st1"), sem("mv1"), sem("ve1"), sem("rs1"), sem("xn_done")
        xT_ps, xT_done = sem("xT_ps"), sem("xT_done")
        gates_ps, gates_done = sem("gates_ps"), sem("gates_done")
        ca_done, cb_done, c_done, tc_done, h_done = sem("ca_done"), sem("cb_done"), sem("c_done"), sem("tc_done"), sem("h_done")
        h_ps, h1_done = sem("h_ps"), sem("h1_done")
        st2, mv2, ve2, rs2, yn_done = sem("st2"), sem("mv2"), sem("ve2"), sem("rs2"), sem("yn_done")
        pay_hi, pay_lo = sem("pay_hi"), sem("pay_lo")
        yT_ps, yT_done = sem("yT_ps"), sem("yT_done")
        logit_ps = sem("logit_ps")
        r_dve, r_exp, r_rank = sem("r_dve"), sem("r_exp"), sem("r_rank")
        slots_done, ids_done, sent_done = sem("slots_done"), sem("ids_done"), sem("sent_done")
        ex_in = [sem(f"ex_in{i}") for i in range(4)]
        ex_hi_done, ex_lo_done = sem("ex_hi_done"), sem("ex_lo_done")
        plan, plan_done = sem("plan"), sem("plan_done")
        pads_sp, pads_act = sem("pads_sp"), sem("pads_act")
        xt_in = [sem(f"xt_in{i}") for i in range(4)]
        in_ps, in_done = sem("in_ps"), sem("in_done")
        up_ps, gelu_done, hhi_done, hlo_done = sem("up_ps"), sem("gelu_done"), sem("hhi_done"), sem("hlo_done")
        down_ps, y_done = sem("down_ps"), sem("y_done")
        dst_p, dst_a, dst_b = sem("dst_p"), sem("dst_a"), sem("dst_b")
        y_out = [sem(f"y_out{i}") for i in range(4)]
        bk_in = [sem(f"bk_in{i}") for i in range(NX)]
        add_a, add_b = sem("add_a"), sem("add_b")
        out_done = sem("out_done")

        N_CONST = 10
        R, R_MASK = 25, 18
        LAST_SLOT = T - 1 + 4

        def slots(eng, step, width, first, start, high, last):
            bodies = (high + 1 - start) // width
            for n in range(first, start):
                step(At(None, n, width))
            with eng.Fori(0, bodies) as i:
                for n in range(start, start + width):
                    step(At(i, n, width))
            for n in range(start + bodies * width, last + 1):
                step(At(None, n, width))

        def slots_a(eng, step, start, high, last=LAST_SLOT):
            slots(eng, step, U, -4, start, high, last)

        def slots_b(eng, step, start, high):
            slots(eng, step, UB, -3, start, high, TILES_B + 1)

        def group_at(n):
            if n.reg is None and n.at == 3:
                return At(None, 0, 1), At(None, 0, U), 1
            if n.at % U == 3 and n.at >= 11:
                return At(n.reg, n.at // U, 1), n - 10, U
            return None

        def through(eng, s, t):
            eng.wait_ge(s, (t + 1).val())

        def wait_alone(eng, s, v):
            v = v if isinstance(v, int) else eng.snap(v)
            eng.wait_ge(const_in, 16 * N_CONST)
            eng.wait_ge(s, v)

        def patches_in(eng, t):
            eng.wait_ge(x_in[(t - 1).mod(NX)], ((t - 1).div(NX) + 1) * 32)

        block = ctx.enter_context(nc.Block())

        @block.sync
        def _(sp):
            for dst, src in ((cst[:, :], const), (biasw[:, :], bias.partition_broadcast(P)),
                             (wih[:, :, :], w_ih), (whh[:, :, :], w_hh), (lbias[:, 0, :], b_ih),
                             (lbias[:, 1, :], b_hh), (rws[:, :], rw),
                             (rbs[:, :, :], rb.partition_broadcast(P)), (h0[:, 3, :], cls.partition_broadcast(P)),
                             (b1s[:, :], b1)):
                sp.dma_start(dst, src).then_inc(const_in, 16)
            sp.dma_start(xraw[NX - 1][:, 0:KC, :], w).then_inc(w_in, 16)
            sp.dma_start(xraw[NX - 1][0:KREST, KC, :], w_rest).then_inc(w_in, 16)

            def step(n):
                t = n + 5
                if t.within(1, T - 1):
                    if t.reg is None and t.at == NX:
                        sp.wait_ge(setup_act, 1)
                        sp.wait_ge(setup_dve, 1)
                    if t.reg is not None or t.at > NX:
                        sp.wait_ge(hi_done, (t - NX).val())
                        sp.wait_ge(lo_done, (t - NX).val())
                    q = (t - 1).mod(NX)
                    row = (t - 1).val() * IN_D
                    sp.dma_start(xraw[q][:, 0:KC, :],
                                 x[bass.ds(row, KC * P), :].rearrange("(p c) b -> p c b", c=KC)
                                 ).then_inc(x_in[q], 16)
                    sp.dma_start(xraw[q][0:KREST, KC, :], x[bass.ds(row + KC * P, KREST), :]
                                 ).then_inc(x_in[q], 16)
                t = n + 3
                if t.within(0, T - 1):
                    if t.reg is not None or t.at >= NP_:
                        through(sp, h0_done, t - NP_)
                    sp.dma_start(posr[:, t.mod(NP_), :],
                                 pos[bass.ds(t.val(), 1), :].rearrange("a h -> (a h)").partition_broadcast(P)
                                 ).then_inc(pos_in[t.mod(NP_)], 16)
                if n.within(0, PIECES - 1):
                    if n.reg is not None or n.at >= 4:
                        through(sp, ex_lo_done, n - 4)
                    sp.dma_start(ex_raw[:, n.mod(4), :], we[:, bass.ds(n.val() * PIECE, PIECE)]
                                 ).then_inc(ex_in[n.mod(4)], 16)

            slots_a(sp, step, 4, T - 6)

            sp.wait_ge(plan_done, 1)
            for e in range(0, E, 2):
                row = sp.value_load(padi[0:1, e:e + 1], min_val=0, max_val=E * CAP - P)
                sp.dma_start(sent[bass.ds(row, P), :], pad[:, :]).then_inc(pads_sp, 16)
            sp.wait_ge(sent_done, 32 * T)
            sp.wait_ge(pads_sp, 16 * E // 2)
            sp.wait_ge(pads_act, 16 * (E // 2 + 1))

            def step_b(n):
                j = n + 3
                if not j.within(0, TILES_B - 1):
                    return
                if j.reg is not None or j.at >= 4:
                    through(sp, in_ps, j - 4)
                    through(sp, dst_b, j - 4)
                    through(sp, y_done, j - 4)
                row = sp.value_load(tabi[0:1, 1, bass.ds(j.val(), 1)], min_val=0, max_val=E * CAP)
                sp.dma_start(xt[j.mod(4)], sent[bass.ds(row, P), :]).then_inc(xt_in[j.mod(4)], 16)
                e = sp.value_load(tabi[0:1, 0, bass.ds(j.val(), 1)], min_val=0, max_val=E - 1)
                sp.dma_start(b2r[:, j.mod(4), :],
                             b2[bass.ds(e, 1), :].rearrange("a h -> (a h)").partition_broadcast(P)
                             ).then_inc(xt_in[j.mod(4)], 16)

            slots_b(sp, step_b, 1, TILES_B - 4)

            for q in range(4):
                sp.wait_ge(y_out[q], 16 * len(range(q, TILES_B, 4)))
            steps = T // CT

            def load(m):
                q = m % NC_
                if m >= NC_:
                    sp.wait_ge(add_b, (m - NC_ + 1) * CT)
                for k in range(2):
                    sp.dma_start(bk[q][:, k * CT:(k + 1) * CT, :],
                                 back[k * TOKENS + m * CT * P:k * TOKENS + (m + 1) * CT * P, :].rearrange(
                                     "(t b) h -> b t h", b=P)).then_inc(bk_in[q], 16)

            for m in range(NC_):
                load(m)
            for m in range(steps):
                sp.wait_ge(add_b, (m + 1) * CT)
                sp.dma_start(out[:, m * CT:(m + 1) * CT, :], h1[:, m * CT:(m + 1) * CT, :]).then_inc(out_done, 16)
                if m + NC_ < steps:
                    load(m + NC_)
            sp.wait_ge(out_done, 16 * steps)

        @block.scalar
        def _(act):
            act.wait_ge(w_in, 32)
            act.activation(whi[:, 0:KC, :], xraw[NX - 1][:, 0:KC, :], ACT.Copy, scale=W_SCALE)
            act.activation(whi[0:KREST, KC, :], xraw[NX - 1][0:KREST, KC, :], ACT.Copy,
                           scale=W_SCALE).then_inc(setup_act, 1)
            act.wait_ge(const_in, 16 * N_CONST)
            act.activation(ident16[:, :], cst[:, C_ID:C_TRI], ACT.Copy)
            act.activation(tri16[:, :], cst[:, C_TRI:C_ONE], ACT.Copy)
            act.activation(ones16[:, :], cst[:, C_ONE:C_IOTA], ACT.Copy)
            act.activation(whh[:, :, :], whh[:, :, :], ACT.Copy, scale=0.5).then_inc(setup_act, 1)
            act.wait_ge(setup_dve, 4)

            def hi(t, a, b):
                q, r = (t - 1).mod(NX), (t - 1).mod(2)
                return act.activation(xhi[r][:, a:b, :], xraw[q][:, a:b, :], ACT.Copy)

            def step(n):
                if n.within(0, T - 1):
                    through(act, gates_ps, n)
                    for g in range(4):
                        last = act.activation(gate[:, g, :], ps_gate[n.mod(2)][:, g * B:(g + 1) * B], ACT.Tanh,
                                              bias=lbias[:, 2, g:g + 1], scale=1.0 if g == 2 else 0.5)
                    last.then_inc(gates_done, 1)
                t = n - 2
                if t.within(0, T - 1):
                    through(act, yT_ps, t)
                    if t.reg is not None or t.at >= 2:
                        through(act, logit_ps, t - 2)
                    act.activation(ynT[:, t.mod(2), :], ps_T[:, P:2 * P], ACT.Copy).then_inc(yT_done, 1)
                t = n + 3
                split = t.within(1, T - 1)
                if split:
                    patches_in(act, t)
                    if t.reg is not None or t.at > 2:
                        act.wait_ge(tok_done, (t - 2).val())
                    hi(t, 0, 9)
                if n.within(0, T - 1):
                    through(act, c_done, n)
                    act.activation(tc[:, :], c2[:, :], ACT.Tanh, scale=0.5).then_inc(tc_done, 1)
                if split:
                    hi(t, 9, KC)
                    q, r = (t - 1).mod(NX), (t - 1).mod(2)
                    act.activation(xhi[r][0:KREST, KC, :], xraw[q][0:KREST, KC, :], ACT.Copy).then_inc(hi_done, 1)
                t = n + 1
                if t.within(0, T - 1):
                    through(act, xT_ps, t)
                    if t.reg is not None or t.at >= 2:
                        through(act, gates_ps, t - 2)
                    act.activation(xnT[:, t.mod(2), :], ps_T[:, 0:P], ACT.Copy).then_inc(xT_done, 1)
                if n.within(0, PIECES - 1):
                    act.wait_ge(ex_in[n.mod(4)], (n.div(4) + 1) * 16)
                    piece = ex_raw[:, n.mod(4), :]
                    flat_hi = ex_hi[:, :, :, :].rearrange("p e m f -> p (e m f)")
                    act.activation(flat_hi[:, bass.ds(n.val() * PIECE, PIECE)], piece, ACT.Copy, scale=E_SCALE)
                    act.activation(piece, piece, ACT.Copy, scale=E_SCALE).then_inc(ex_hi_done, 1)
                at = group_at(n)
                if at:
                    g, t0, m = at
                    act.wait_ge(r_dve, g.val() * R + 3)
                    act.activation(pr[:, 0:m, :], lg[:, 0:m, :], ACT.Exp).then_inc(r_exp, 1)

            slots_a(act, step, 5, T - 4)

            act.wait_ge(plan_done, 1)
            act.dma_start(sent[E * CAP:E * CAP + P, :], pad[:, :]).then_inc(pads_act, 16)
            for e in range(1, E, 2):
                row = act.value_load(padi[0:1, e:e + 1], min_val=0, max_val=E * CAP - P)
                act.dma_start(sent[bass.ds(row, P), :], pad[:, :]).then_inc(pads_act, 16)

            def step_b(n):
                j = n + 1
                if j.within(0, TILES_B - 1):
                    through(act, in_ps, j)
                    if j.reg is not None or j.at >= 2:
                        through(act, up_ps, j - 2)
                    act.activation(xTs[j.mod(2)], ps_in[j.mod(2)], ACT.Copy).then_inc(in_done, 1)
                if n.within(0, TILES_B - 1):
                    e = act.value_load(tabi[0:1, 0, bass.ds(n.val(), 1)], min_val=0, max_val=E - 1)
                    through(act, up_ps, n)
                    if n.reg is not None or n.at >= 2:
                        through(act, hlo_done, n - 2)
                    for c in range(FC):
                        last = act.activation(hf[n.mod(2)][:, c * P:(c + 1) * P],
                                              ps_up[n.mod(2)][:, c * P:(c + 1) * P], ACT.Gelu,
                                              bias=b1s[:, bass.ds(e * FC + c, 1)], scale=1.0 / E_SCALE)
                    last.then_inc(gelu_done, 1)

            slots_b(act, step_b, 2, TILES_B - 2)

        @block.vector
        def _(dve):
            dve.wait_ge(w_in, 32)
            dve.wait_ge(setup_act, 1)
            dve.scalar_tensor_tensor(wlo[:, 0:KC, :].rearrange("p a b -> p (a b)"),
                                     xraw[NX - 1][:, 0:KC, :].rearrange("p a b -> p (a b)"), W_SCALE,
                                     whi[:, 0:KC, :].rearrange("p a b -> p (a b)"), ALU.mult, ALU.subtract)
            dve.scalar_tensor_tensor(wlo[0:KREST, KC, :], xraw[NX - 1][0:KREST, KC, :], W_SCALE,
                                     whi[0:KREST, KC, :], ALU.mult, ALU.subtract).then_inc(setup_dve, 1)
            dve.memset(c2[:, :], 0.0)
            dve.memset(slot[:, :, :], 0)
            dve.memset(h2[:, 1, :], 0.0).then_inc(setup_dve, 1)
            dve.wait_ge(const_in, 16 * N_CONST)
            dve.tensor_scalar(biasw[:, :], biasw[:, :], W_SCALE, None, ALU.mult)
            dve.tensor_copy(count[:, :], cst[:, C_EBASE:C_TOK])
            dve.tensor_tensor(lbias[:, 2, :], lbias[:, 0, :], lbias[:, 1, :], ALU.add).then_inc(setup_dve, 1)
            dve.wait_ge(setup_dve, 3)
            dve.tensor_tensor(lbias[:, 2, :], lbias[:, 2, :], cst[:, C_BSC:C_POW], ALU.mult).then_inc(setup_dve, 1)

            def normed(which, t, src, dst, s_st, s_mv, s_ve, s_rs, s_out):
                def a():
                    dve.bn_stats(stats[:, which, :], src).then_inc(s_st, 1)

                def b():
                    wait_alone(dve, s_st, (t + 1).val())
                    dve.bn_aggr(mv[:, which, :], stats[:, which, :]).then_inc(s_mv, 1)

                def c():
                    through(dve, s_mv, t)
                    dve.tensor_scalar(veps[:, which:which + 1], mv[:, which, 1:2], EPS, None,
                                      ALU.add).then_inc(s_ve, 1)

                def d():
                    through(dve, s_rs, t)
                    dve.tensor_scalar(dst, src, mv[:, which, 0:1], rstd[:, which:which + 1], ALU.subtract,
                                      ALU.mult).then_inc(s_out, 1)
                return a, b, c, d

            def lo(t, a, b):
                q, r = (t - 1).mod(NX), (t - 1).mod(2)
                dve.tensor_tensor(xlo[r][:, a:b, :], xraw[q][:, a:b, :], xhi[r][:, a:b, :], ALU.subtract)

            def step(n):
                ln1 = ln2 = None
                if group_at(n):
                    route_logits(*group_at(n))
                t = n + 1
                if t.within(0, T - 1):
                    q = t.mod(4)
                    dve.wait_ge(pos_in[t.mod(NP_)], (t.div(NP_) + 1) * 16)
                    if t.reg is None and t.at == 0:
                        dve.tensor_tensor(h0[:, 0, :], h0[:, 3, :], posr[:, 0, :], ALU.mult).then_inc(h0_done, 1)
                        dve.wait_ge(setup_dve, 4)
                        dve.tensor_copy(tok_sum[:, :], biasw[:, :]).then_inc(biased, 1)
                    else:
                        dve.wait_ge(tok_done, t.val())
                        dve.tensor_tensor(tok_sum[:, :], ps_tok[t.mod(2)][:, 0:HID], biasw[:, :],
                                          ALU.add).then_inc(biased, 1)
                        through(dve, biased, t)
                        dve.scalar_tensor_tensor(h0[:, q, :], tok_sum[:, :], 1.0 / W_SCALE, posr[:, t.mod(NP_), :],
                                                 ALU.mult, ALU.mult).then_inc(h0_done, 1)
                    through(dve, h0_done, t)
                    ln1 = normed(0, t, h0[:, q, :], xn[:, t.mod(2), :], st1, mv1, ve1, rs1, xn_done)
                    ln1[0]()
                    ln1[1]()
                    ln1[2]()
                t = n - 1
                if t.within(0, T - 1):
                    through(dve, h_ps, t)
                    row = h1[:, bass.ds(t.val(), 1), :].rearrange("p a h -> p (a h)")
                    dve.scalar_tensor_tensor(row, ps_h[:, 0:P], 0.5, h0[:, t.mod(4), :], ALU.mult,
                                             ALU.add).then_inc(h1_done, 1)
                    ln2 = normed(1, t, row, yn[:, t.mod(NY), :], st2, mv2, ve2, rs2, yn_done)
                if ln1:
                    if n.reg is not None or n.at >= 1:
                        through(dve, xT_ps, n - 1)
                    ln1[3]()
                if ln2:
                    wait_alone(dve, h1_done, (t + 1).val())
                    ln2[0]()
                    ln2[1]()
                if n.within(0, T - 1):
                    through(dve, gates_done, n)
                    dve.scalar_tensor_tensor(ca[:, :], gate[:, 1, :], 1.0, c2[:, :], ALU.add,
                                             ALU.mult).then_inc(ca_done, 1)
                    dve.scalar_tensor_tensor(cb[:, :], gate[:, 0, :], 1.0, gate[:, 2, :], ALU.add,
                                             ALU.mult).then_inc(cb_done, 1)
                if ln2:
                    ln2[2]()
                if n.within(0, T - 1):
                    through(dve, ca_done, n)
                    through(dve, cb_done, n)
                    dve.scalar_tensor_tensor(c2[:, :], ca[:, :], 0.5, cb[:, :], ALU.mult, ALU.add).then_inc(c_done, 1)
                if ln2:
                    if t.reg is not None or t.at >= NY:
                        through(dve, pay_lo, t - NY)
                        through(dve, yT_ps, t - NY)
                    ln2[3]()
                t = n + 3
                split = t.within(1, T - 1)
                if split:
                    dve.wait_ge(hi_done, t.val())
                    lo(t, 0, 9)
                if n.within(0, T - 1):
                    through(dve, tc_done, n)
                    dve.scalar_tensor_tensor(h2[:, n.mod(2), :], gate[:, 3, :], 1.0, tc[:, :], ALU.add,
                                             ALU.mult).then_inc(h_done, 1)
                if split:
                    lo(t, 9, KC)
                    q, r = (t - 1).mod(NX), (t - 1).mod(2)
                    dve.tensor_tensor(xlo[r][0:KREST, KC, :], xraw[q][0:KREST, KC, :], xhi[r][0:KREST, KC, :],
                                      ALU.subtract).then_inc(lo_done, 1)
                if group_at(n):
                    route_masks(*group_at(n))
                if group_at(n - 1):
                    route_slots(*group_at(n - 1))

            def route_logits(g, t0, m):
                dve.wait_ge(logit_ps, (t0 + m).val())
                if g.reg is not None or g.at >= 1:
                    dve.wait_ge(r_dve, g.val() * R)
                dve.tensor_tensor(lg[:, 0:m, :], ps_logit[:, 0:m * E].rearrange("p (t e) -> p t e", e=E),
                                  rbs[:, 0:m, :], ALU.add).then_inc(r_dve, 1)

            def route_masks(g, t0, m):
                count_of = [1]

                def by(ins):
                    ins.then_inc(r_dve, 1)
                    count_of[0] += 1

                def seen():
                    dve.wait_ge(r_dve, g.val() * R + count_of[0])

                def wide(row):
                    return row.unsqueeze(2).to_broadcast([P, m, E])

                def lines(a):
                    return a.rearrange("p t e -> p (t e)")

                L, Q, Q2, K = (a[:, 0:m, :] for a in (lg, pr, pr2, cand))
                OH = [oh[:, k, 0:m, :] for k in range(2)]
                iota = cst[:, C_IOTA:C_IOTA + m * E].rearrange("p (t e) -> p t e", e=E)
                most = [gates[:, k, bass.ds(t0.val(), m)] for k in range(2)]
                first_of = first[:, bass.ds(t0.val(), m)]
                seen()
                by(dve.tensor_reduce(red[:, 0, 0:m], L, AX.X, ALU.max))
                seen()
                by(dve.tensor_tensor(L, L, wide(red[:, 0, 0:m]), ALU.subtract))
                dve.wait_ge(r_exp, (g + 1).val())
                by(dve.tensor_reduce(red[:, 1, 0:m], Q, AX.X, ALU.add))
                seen()
                by(dve.reciprocal(red[:, 2, 0:m], red[:, 1, 0:m]))
                seen()
                by(dve.tensor_tensor(Q, Q, wide(red[:, 2, 0:m]), ALU.mult))
                seen()
                which = (first_of, red[:, 3, 0:m])
                for k, q in enumerate((Q, Q2)):
                    by(dve.tensor_reduce(most[k], q, AX.X, ALU.max))
                    seen()
                    by(dve.tensor_tensor(L, q, wide(most[k]), ALU.is_lt))
                    seen()
                    by(dve.scalar_tensor_tensor(lines(K), lines(L), float(E), lines(iota), ALU.mult, ALU.add))
                    seen()
                    by(dve.tensor_reduce(which[k], K, AX.X, ALU.min))
                    seen()
                    by(dve.tensor_tensor(OH[k], iota, wide(which[k]), ALU.is_equal))
                    seen()
                    if k == 0:
                        by(dve.scalar_tensor_tensor(lines(Q2), lines(OH[0]), -2.0, lines(Q), ALU.mult, ALU.add))
                        seen()
                by(dve.tensor_tensor(mask16[:, 0:m, :], OH[0], OH[1], ALU.add))
                assert count_of[0] == R_MASK

            def route_slots(g, t0, m):
                count_of = [R_MASK]

                def by(ins):
                    ins.then_inc(r_dve, 1)
                    count_of[0] += 1

                def seen():
                    dve.wait_ge(r_dve, g.val() * R + count_of[0])

                K, Q2 = cand[:, 0:m, :], pr2[:, 0:m, :]
                OH = [oh[:, k, 0:m, :] for k in range(2)]
                dve.wait_ge(r_rank, (g + 1).val())
                by(dve.tensor_tensor(rank[:, 0:m, :], ps_rank[:, 0:m * E].rearrange("p (t e) -> p t e", e=E),
                                     count[:, :].unsqueeze(1).to_broadcast([P, m, E]), ALU.add))
                seen()
                by(dve.tensor_tensor(count[:, :], count[:, :], ps_rank[:, P:P + E], ALU.add))
                seen()
                by(dve.tensor_tensor(K, rank[:, 0:m, :], OH[0], ALU.mult))
                by(dve.tensor_tensor(Q2, rank[:, 0:m, :], OH[1], ALU.mult))
                seen()
                by(dve.tensor_reduce(slotf[:, 0, 0:m], K, AX.X, ALU.add))
                by(dve.tensor_reduce(slotf[:, 1, 0:m], Q2, AX.X, ALU.add))
                seen()
                if g.reg is not None or g.at >= 1:
                    dve.wait_ge(ids_done, g.val())
                by(dve.tensor_copy(slot[:, :, 0:m], slotf[:, :, 0:m]))
                assert count_of[0] == R

            slots_a(dve, step, 1 + NY, T - 4)

            done = [0]

            def by(ins):
                ins.then_inc(plan, 1)
                done[0] += 1

            def seen():
                dve.wait_ge(plan, done[0])

            dve.wait_ge(r_dve, R * (1 + (T - 1) // U))
            by(dve.tensor_copy(padi[:, :], count[0:1, :]))
            by(dve.tensor_tensor(tabs[:, 0, :], count[:, :], cst[:, C_EBASE:C_TOK], ALU.subtract))
            by(dve.memset(pad[:, :], 0.0))
            seen()
            by(dve.memset(pad[:, HID:HID + 1].bitcast(I32), NO_TOKEN))
            whole = [tabs[:, k, :].bitcast(I32) for k in (1, 2)]
            by(dve.tensor_scalar(whole[0], tabs[:, 0, :], float(P - 1), None, ALU.add))
            seen()
            by(dve.tensor_scalar(whole[1], whole[0], 7, 7, ALU.logical_shift_right, ALU.logical_shift_left))
            seen()
            by(dve.tensor_copy(tabs[:, 3, :], whole[1]))
            seen()
            length, row = tabs[:, 3, :], 3
            for k in (1, 2, 4, 8):
                by(dve.tensor_tensor(tabs[:, row + 1, k:E], tabs[:, row, k:E], tabs[:, row, 0:E - k], ALU.add))
                by(dve.tensor_copy(tabs[:, row + 1, 0:k], tabs[:, row, 0:k]))
                seen()
                row += 1
            ends = tabs[:, row, :]
            start_j = cst[:, C_J:C_END]
            over = big.rearrange("p (j e) -> p j e", e=E)
            over2 = big2.rearrange("p (j e) -> p j e", e=E)
            by(dve.tensor_tensor(over, start_j.unsqueeze(2).to_broadcast([P, TILES_B, E]),
                                 ends.unsqueeze(1).to_broadcast([P, TILES_B, E]), ALU.is_ge))
            seen()
            by(dve.tensor_reduce(tabj[:, 0, :], over, AX.X, ALU.add))
            by(dve.tensor_tensor(over2, over, length.unsqueeze(1).to_broadcast([P, TILES_B, E]), ALU.mult))
            seen()
            by(dve.tensor_reduce(tabj[:, 1, :], over2, AX.X, ALU.add))
            by(dve.tensor_scalar(tabj[:, 2, :], tabj[:, 0, :], float(CAP), None, ALU.mult))
            seen()
            by(dve.tensor_tensor(tabj[:, 1, :], start_j, tabj[:, 1, :], ALU.subtract))
            by(dve.tensor_scalar(tabj[:, 0, :], tabj[:, 0, :], float(E - 1), None, ALU.min))
            seen()
            by(dve.tensor_tensor(tabj[:, 1, :], tabj[:, 1, :], tabj[:, 2, :], ALU.add))
            by(dve.tensor_copy(tabi[:, 0, :], tabj[0:1, 0, :]))
            seen()
            dve.tensor_scalar(tabi[:, 1, :], tabj[0:1, 1, :], float(E * CAP), None, ALU.min).then_inc(plan_done, 1)

            def step_b(n):
                j = n
                if j.within(0, TILES_B - 1):
                    q = j.mod(4)
                    dve.wait_ge(xt_in[q], (j.div(4) + 1) * 32)
                    if j.reg is not None or j.at >= 4:
                        dve.wait_ge(y_out[q], j.div(4) * 16)
                    dve.tensor_scalar(dsto[q], xt[q][:, HID + 1:HID + 2], tabj[:, 0, bass.ds(j.val(), 1)],
                                      float(TOKENS), ALU.not_equal, ALU.mult).then_inc(dst_a, 1)
                    through(dve, gelu_done, j)
                    if j.reg is not None or j.at >= 2:
                        through(dve, down_ps, j - 2)
                    dve.tensor_copy(hhi[j.mod(2)], hf[j.mod(2)]).then_inc(hhi_done, 1)
                    through(dve, hhi_done, j)
                    dve.tensor_tensor(hlo[j.mod(2)], hf[j.mod(2)], hhi[j.mod(2)], ALU.subtract).then_inc(hlo_done, 1)
                j = n - 1
                if j.within(0, TILES_B - 1):
                    q = j.mod(4)
                    through(dve, down_ps, j)
                    dve.scalar_tensor_tensor(yo[q], ps_down[j.mod(2)][:, 0:HID], 1.0 / E_SCALE,
                                             b2r[:, q, :], ALU.mult, ALU.add).then_inc(y_done, 1)

            slots_b(dve, step_b, 5, TILES_B - 1)

            for m in range(T // CT):
                q = m % NC_
                dve.wait_ge(bk_in[q], 32 * (m // NC_ + 1))
                for k, s in ((0, add_a), (1, add_b)):
                    for i in range(CT):
                        t = m * CT + i
                        if k == 1:
                            dve.wait_ge(add_a, t + 1)
                        dve.scalar_tensor_tensor(h1[:, t, :], bk[q][:, k * CT + i, :], gates[:, k, t:t + 1],
                                                 h1[:, t, :], ALU.mult, ALU.add).then_inc(s, 1)

        @block.gpsimd
        def _(pool):
            pool.wait_ge(const_in, 16 * N_CONST)

            def inverse_root(which, t, s_ve, s_rs):
                through(pool, s_ve, t)
                pool.tensor_tensor(rstd[:, which:which + 1], veps[:, which:which + 1], cst[:, C_POW:C_POW + 1],
                                   ALU.pow).then_inc(s_rs, 1)

            def step(n):
                sent_t = n - 12
                sends = sent_t.within(0, T - 1)
                if sends:
                    if sent_t.reg is None and sent_t.at == 0:
                        g, col = At(None, 0, 1), 0
                    else:
                        g, col = At(sent_t.reg, (sent_t.at - 1) // U + 1, 1), (sent_t.at - 1) % U
                    if col == 0:
                        pool.wait_ge(r_dve, (g.val() + 1) * R)
                t = n + 1
                if t.within(0, T - 1):
                    inverse_root(0, t, ve1, rs1)
                if sends:
                    if col == 0:
                        pool.tensor_copy(slot_own[:, :, :], slot[:, :, :]).then_inc(ids_done, 1)
                    pool.tensor_copy(pay[:, sent_t.mod(NY), HID + 1:HID + 2],
                                     first[:, bass.ds(sent_t.val(), 1)]).then_inc(dst_p, 1)
                    pool.wait_ge(ids_done, (g + 1).val())
                    through(pool, dst_p, sent_t)
                    through(pool, pay_lo, sent_t)
                t = n - 1
                if t.within(0, T - 1):
                    inverse_root(1, t, ve2, rs2)
                if sends:
                    for k in range(2):
                        pool.indirect_dma_start(
                            sent, bass.IndirectOffsetOnAxis(ap=slot_own[:, k, col:col + 1], axis=0),
                            pay[:, sent_t.mod(NY), :], None, bounds_check=E * CAP - 1, oob_is_err=False
                        ).then_inc(sent_done, 16)
                t = n - 4
                packs = t.within(0, T - 1)
                if packs:
                    through(pool, yn_done, t)
                    if t.reg is not None or t.at >= NY:
                        pool.wait_ge(sent_done, (t - NY + 1).val() * 32)
                if n.within(0, PIECES - 1):
                    through(pool, ex_hi_done, n)
                    flat_hi = ex_hi[:, :, :, :].rearrange("p e m f -> p (e m f)")
                    flat_lo = ex_lo[:, :, :, :].rearrange("p e m f -> p (e m f)")
                    here = bass.ds(n.val() * PIECE, PIECE)
                    pool.tensor_tensor(flat_lo[:, here], ex_raw[:, n.mod(4), :], flat_hi[:, here],
                                       ALU.subtract).then_inc(ex_lo_done, 1)
                if packs:
                    q = t.mod(NY)
                    halves = pay[:, q, 0:HID].bitcast(F16)
                    pool.tensor_copy(halves[:, 0:HID], yn[:, q, :]).then_inc(pay_hi, 1)
                    pool.tensor_copy(pay[:, q, HID:HID + 1].bitcast(I32), cst[:, bass.ds(t.val() + C_TOK, 1)])
                    through(pool, pay_hi, t)
                    pool.tensor_tensor(halves[:, HID:2 * HID], yn[:, q, :], halves[:, 0:HID],
                                       ALU.subtract).then_inc(pay_lo, 1)

            slots_a(pool, step, 13, PIECES - 1, T - 1 + 12)

            def step_b(n):
                j = n - 1
                sends = j.within(0, TILES_B - 1)
                if sends:
                    through(pool, dst_b, j)
                    through(pool, y_done, j)
                if n.within(0, TILES_B - 1):
                    through(pool, dst_a, n)
                    q = n.mod(4)
                    pool.tensor_tensor(dsti[q], dsto[q], xt[q][:, HID:HID + 1].bitcast(I32), ALU.add).then_inc(dst_b, 1)
                if sends:
                    q = j.mod(4)
                    pool.indirect_dma_start(back, bass.IndirectOffsetOnAxis(ap=dsti[q], axis=0), yo[q], None,
                                            bounds_check=2 * TOKENS - 1, oob_is_err=False).then_inc(y_out[q], 16)

            pool.wait_ge(plan_done, 1)
            slots_b(pool, step_b, 5, TILES_B - 1)

        @block.tensor
        def _(pe):
            pe.wait_ge(setup_act, 2)
            pe.wait_ge(setup_dve, 4)
            ident = cst[:, C_ID:C_TRI]

            def project(t, a, b):
                r = (t - 1).mod(2)
                for c in range(a, b):
                    rows = slice(0, P if c < KC else KREST)
                    for k, (l, w_) in enumerate(((xhi, whi), (xhi, wlo), (xlo, whi))):
                        last = pe.matmul(ps_tok[t.mod(2)][:, 0:HID], l[r][rows, c, :], w_[rows, c, :],
                                         start=(c == 0 and k == 0), stop=(c == KC and k == 2))
                return last

            def step(n):
                if n.within(0, T - 1):
                    if n.reg is not None or n.at >= 1:
                        through(pe, h_done, n - 1)
                    for g in range(4):
                        last = pe.matmul(ps_gate[n.mod(2)][:, g * B:(g + 1) * B], whh[:, g, :],
                                         h2[:, (n - 1).mod(2), :], start=False, stop=True, skip_group_check=True)
                    last.then_inc(gates_ps, 1)
                t = n - 1
                if t.within(0, T - 1):
                    through(pe, h_done, t)
                    if t.reg is not None or t.at >= 1:
                        through(pe, h1_done, t - 1)
                    pe.transpose(ps_h[:, 0:P], h2[:, t.mod(2), :], ident).then_inc(h_ps, 1)
                t = n + 2
                proj = t.within(1, T - 1)
                if proj:
                    pe.wait_ge(lo_done, t.val())
                    if t.reg is not None or t.at > 2:
                        through(pe, h0_done, t - 2)
                    project(t, 0, 10)
                t = n + 1
                if t.within(0, T - 1):
                    through(pe, xn_done, t)
                    if t.reg is not None or t.at >= 3:
                        through(pe, yT_done, t - 3)
                    pe.transpose(ps_T[:, 0:P], xn[:, t.mod(2), :], ident).then_inc(xT_ps, 1)
                at = group_at(n - 1)
                if at:
                    g, t0, m = at
                    pe.wait_ge(r_dve, g.val() * R + R_MASK)
                    pe.matmul(ps_rank[:, 0:m * E], tri16[:, :], mask16[:, 0:m, :], start=True, stop=False,
                              skip_group_check=True)
                    for k in range(1, m):
                        pe.matmul(ps_rank[:, k * E:m * E], ones16[:, :], mask16[:, 0:m - k, :], start=False,
                                  stop=False, skip_group_check=True)
                    for k in range(m):
                        last = pe.matmul(ps_rank[:, P:P + E], ones16[:, :], mask16[:, k, :], start=False,
                                         stop=True, skip_group_check=True)
                    last.then_inc(r_rank, 1)
                if proj:
                    project(n + 2, 10, KC + 1).then_inc(tok_done, 1)
                if t.within(0, T - 1):
                    through(pe, xT_done, t)
                    if t.reg is not None or t.at >= 2:
                        through(pe, gates_done, t - 2)
                    for g in range(4):
                        pe.matmul(ps_gate[t.mod(2)][:, g * B:(g + 1) * B], wih[:, g, :], xnT[:, t.mod(2), :],
                                  start=(g == 0), stop=False, skip_group_check=True)
                t = n - 1
                if t.within(0, T - 1):
                    through(pe, yn_done, t)
                    if (t + 2).within(0, T - 1):
                        through(pe, xT_done, t + 2)
                    if t.reg is not None or t.at >= 1:
                        through(pe, yT_done, t - 1)
                    pe.transpose(ps_T[:, P:2 * P], yn[:, t.mod(NY), :], ident).then_inc(yT_ps, 1)
                t = n - 2
                if t.within(0, T - 1):
                    through(pe, yT_done, t)
                    if t.reg is None and t.at == 0:
                        col = 0
                    else:
                        col = (t.at - 1) % U
                        if col == 0:
                            g = At(t.reg, (t.at - 1) // U, 1)
                            pe.wait_ge(r_dve, g.val() * R + 1)
                    pe.matmul(ps_logit[:, col * E:(col + 1) * E], ynT[:, t.mod(2), :], rws[:, :], start=True,
                              stop=True).then_inc(logit_ps, 1)
            slots_a(pe, step, 5, T - 3)
            pe.wait_ge(plan_done, 1)
            pe.wait_ge(ex_lo_done, PIECES)
            pe.wait_ge(gates_done, T)
            pe.wait_ge(yT_done, T)

            def step_b(n):
                j = n + 1
                if j.within(0, TILES_B - 1):
                    pe.wait_ge(xt_in[j.mod(4)], (j.div(4) + 1) * 32)
                    if j.reg is not None or j.at >= 2:
                        through(pe, in_done, j - 2)
                    halves = xt[j.mod(4)][:, 0:HID].bitcast(F16)
                    for k in range(2):
                        last = pe.transpose(ps_in[j.mod(2)][:, k * P:(k + 1) * P], halves[:, k * P:(k + 1) * P],
                                            ident16[:, :])
                    last.then_inc(in_ps, 1)
                if n.within(0, TILES_B - 1):
                    e = pe.value_load(tabi[0:1, 0, bass.ds(n.val(), 1)], min_val=0, max_val=E - 1)
                    through(pe, in_done, n)
                    if n.reg is not None or n.at >= 2:
                        through(pe, gelu_done, n - 2)
                    x_hi, x_lo = xTs[n.mod(2)][:, 0:P], xTs[n.mod(2)][:, P:2 * P]
                    for c in range(FC):
                        for k, (w_, r) in enumerate(((ex_hi, x_hi), (ex_hi, x_lo), (ex_lo, x_hi))):
                            w1 = w_[:, bass.ds(e, 1), 0, c * P:(c + 1) * P].rearrange("p a f -> p (a f)")
                            last = pe.matmul(ps_up[n.mod(2)][:, c * P:(c + 1) * P], w1, r, start=(k == 0),
                                             stop=(k == 2))
                    last.then_inc(up_ps, 1)
                j = n - 1
                if j.within(0, TILES_B - 1):
                    e = pe.value_load(tabi[0:1, 0, bass.ds(j.val(), 1)], min_val=0, max_val=E - 1)
                    through(pe, hlo_done, j)
                    if j.reg is not None or j.at >= 2:
                        through(pe, y_done, j - 2)
                    for c in range(FC):
                        for k, (h_, w_) in enumerate(((hhi, ex_hi), (hhi, ex_lo), (hlo, ex_hi))):
                            w2 = w_[:, bass.ds(e, 1), 1, c * HID:(c + 1) * HID].rearrange("p a f -> p (a f)")
                            last = pe.matmul(ps_down[j.mod(2)][:, 0:HID], h_[j.mod(2)][:, c * P:(c + 1) * P], w2,
                                             start=(c == 0 and k == 0), stop=(c == FC - 1 and k == 2))
                    last.then_inc(down_ps, 1)

            slots_b(pe, step_b, 3, TILES_B - 2)


def kernel(**inputs):
    import concourse.bacc as bacc
    from concourse.bass_utils import run_bass_kernel_spmd as run

    a = {k: np.asarray(v) for k, v in inputs.items()}

    def whole(v):
        return np.ascontiguousarray(v)

    x = a["x"].reshape(B, C, GRID, PATCH, GRID, PATCH).transpose(2, 4, 1, 3, 5, 0)
    w = a["L0_tok_W"].T
    w1 = a["L0_ffn_w1"].transpose(2, 0, 1)
    w2 = a["L0_ffn_w2"].reshape(E, HID, FC, P).transpose(3, 0, 2, 1)
    arrays = {
        "x": whole(x).reshape((T - 1) * IN_D, B),
        "w": whole(w[:KC * P]).reshape(P, KC, HID),
        "w_rest": whole(w[KC * P:]),
        "bias": whole(a["L0_tok_b"]),
        "cls": whole(a["L0_tok_class_token"]).reshape(HID),
        "pos": whole(a["L0_tok_pos_embed"]),
        "w_ih": whole(a["L0_attn_W_ih"].reshape(4, HID, HID).transpose(2, 0, 1)),
        "w_hh": whole(a["L0_attn_W_hh"].reshape(4, HID, HID).transpose(2, 0, 1)),
        "b_ih": whole(a["L0_attn_b_ih"].reshape(4, HID).T),
        "b_hh": whole(a["L0_attn_b_hh"].reshape(4, HID).T),
        "rw": whole(a["L0_ffn_router_w"].T),
        "rb": whole(np.broadcast_to(a["L0_ffn_router_b"], (U, E))),
        "we": whole(np.stack([w1, w2.reshape(P, E, FC * HID)], axis=2)).reshape(P, E * 2 * FF),
        "b1": whole(a["L0_ffn_b1"].reshape(E, FC, P).transpose(2, 0, 1)).reshape(P, E * FC),
        "b2": whole(a["L0_ffn_b2"]),
        "const": constants(),
    }
    nc = bacc.Bacc("TRN2", target_bir_lowering=False, num_devices=1)
    args = {k: nc.dram_tensor(f"in_{k}", list(v.shape), mybir.dt.from_np(v.dtype), kind="ExternalInput").ap()
            for k, v in arrays.items()}
    out = nc.dram_tensor("out_tower", [B, T, HID], mybir.dt.float32, kind="ExternalOutput").ap()
    tower(nc, out=out, **args)
    r = run(nc, [{f"in_{k}": v for k, v in arrays.items()}], core_ids=[0])
    return r.results[0]["out_tower"]
```

```python
from contextlib import ExitStack

import numpy as np

import concourse.bass as bass
from concourse import mybir

P = 128
B, C, IMG, GRID, HID = 128, 3, 224, 8, 128
PATCH = IMG // GRID
IN_D = C * PATCH * PATCH
T = GRID * GRID + 1
KC = IN_D // P
KREST = IN_D - KC * P
KBIAS = 64
KS = 9
E, FF = 16, 512
FC = FF // P
TOKENS = T * B
HALVES = 2
ROWS = HALVES * P
CAP = TOKENS + ROWS
TILES_B = (2 * TOKENS - E) // ROWS + E
ROW = HID + 2
EPS = 1e-5
W_SCALE = 1024.0
E_SCALE = 256.0
PIECE = 256
PIECES = E * 2 * FF // PIECE
U = 8
UB = 4
NX = 4
NPOS = 4
NY = 8
NO_TOKEN = 1 << 20
CT = 5

C_ID, C_TRI, C_ONE, C_IOTA, C_EBASE, C_TOK, C_BSC, C_POW, C_J = np.cumsum([0, P, P, P, U * E, E, T, 4, 1]).tolist()
C_END = C_J + TILES_B


def constants():
    c = np.zeros((P, C_END), np.float32)
    c[:, C_ID:C_TRI] = np.eye(P)
    c[:, C_TRI:C_ONE] = np.triu(np.ones((P, P)), 1)
    c[:, C_ONE:C_IOTA] = 1.0
    c[:, C_IOTA:C_EBASE] = np.tile(np.arange(E), U)
    c[:, C_EBASE:C_TOK] = np.arange(E) * CAP
    c[:, C_TOK:C_BSC] = np.arange(P)[:, None] + P * np.arange(T)
    c[:, C_POW] = -0.5
    c[:, C_BSC:C_POW] = [0.5, 0.5, 1.0, 0.5]
    c[:, C_J:] = ROWS * np.arange(TILES_B)
    return c


class At:

    def __init__(self, reg, at, width):
        self.reg, self.at, self.width = reg, at, width

    def __add__(self, k):
        return At(self.reg, self.at + k, self.width)

    def __sub__(self, k):
        return self + -k

    def within(self, low, high):
        return self.reg is not None or low <= self.at <= high

    def val(self):
        return self.at if self.reg is None else self.reg * self.width + self.at

    def mod(self, m):
        assert self.width % m == 0 or self.reg is None
        return self.at % m

    def div(self, m):
        assert self.width % m == 0 or self.reg is None
        return self.at // m if self.reg is None else self.reg * (self.width // m) + self.at // m


def tower(nc, x, w, w_rest, cls, pos, w_ih, w_hh, b_ih, b_hh, rw, rb, we, b1, b2, const, out):
    F32, F16, I32 = mybir.dt.float32, mybir.dt.float16, mybir.dt.int32
    ALU, ACT, AX = mybir.AluOpType, mybir.ActivationFunctionType, mybir.AxisListType
    ctx = ExitStack()
    with ctx:
        def sb(name, shape, dt=F32):
            return ctx.enter_context(nc.sbuf_tensor(name, shape, dt))

        def sem(name):
            return ctx.enter_context(nc.semaphore(name))

        sent = nc.dram_tensor("sent", [E * CAP + ROWS, ROW], F32, kind="Internal").ap()
        back = nc.dram_tensor("back", [2 * TOKENS, HID], F32, kind="Internal").ap()

        cst = sb("cst", [P, C_END])
        ident16 = sb("ident16", [P, P], F16)
        tri16 = sb("tri16", [P, P], F16)
        ones16 = sb("ones16", [P, P], F16)
        patches = sb("patches", [P, NX, KC + 1, P])
        xraw = [patches[:, i] for i in range(NX)]
        xhi = [sb(f"xhi{i}", [P, KS, P], F16) for i in range(2)]
        xlo = [sb(f"xlo{i}", [P, KS, P], F16) for i in range(2)]
        ws = sb("ws", [P, KC + 1, HID])
        whi = sb("whi", [P, KS, HID], F16)
        wlo = sb("wlo", [P, KS, HID], F16)
        posr = sb("posr", [P, NPOS, HID])
        wih = sb("wih", [HID, 4, HID])
        whh = sb("whh", [HID, 4, HID])
        lbias = sb("lbias", [HID, 3, 4])
        rws = sb("rws", [HID, E])
        rbs = sb("rbs", [P, U, E])
        ex_hi = sb("ex_hi", [P, E, 2, FF], F16)
        ex_lo = sb("ex_lo", [P, E, 2, FF], F16)
        ex_raw = sb("ex_raw", [P, 4, PIECE])
        b1s = sb("b1s", [P, E * FC])
        b2r = sb("b2r", [P, 4, HID])
        h0 = sb("h0", [P, 4, HID])
        stats = sb("stats", [P, 2, 6])
        mv = sb("mv", [P, 2, 2])
        veps = sb("veps", [P, 2])
        rstd = sb("rstd", [P, 2])
        xn = sb("xn", [P, 2, HID])
        xnT = sb("xnT", [HID, 2, B])
        gate = sb("gate", [HID, 4, B])
        c2 = sb("c2", [HID, B])
        ca = sb("ca", [HID, B])
        cb = sb("cb", [HID, B])
        tc = sb("tc", [HID, B])
        h2 = sb("h2", [HID, 2, B])
        h1 = sb("h1", [P, T, HID])
        yn = sb("yn", [P, NY, HID])
        ynT = sb("ynT", [HID, 2, B])
        pay = sb("pay", [P, NY, ROW])
        lg = sb("lg", [P, U, E])
        pr = sb("pr", [P, U, E])
        pr2 = sb("pr2", [P, U, E])
        cand = sb("cand", [P, U, E])
        oh = sb("oh", [P, 2, U, E])
        mask16 = sb("mask16", [P, U, E], F16)
        rank = sb("rank", [P, U, E])
        red = sb("red", [P, 8, U])
        gates = sb("gates", [P, 2, T])
        first = sb("first", [P, T])
        count = sb("count", [P, E])
        slotf = sb("slotf", [P, 2, U])
        slot = sb("slot", [P, 2, U], I32)
        slot_own = sb("slot_own", [P, 2, U], I32)
        tabs = sb("tabs", [P, 12, E])
        tabi = sb("tabi", [1, 2, TILES_B], I32)
        padi = sb("padi", [1, E], I32)
        pad = sb("pad", [P, HALVES, ROW])

        arena = patches[:, :, :, :].rearrange("p q c b -> p (q c b)")
        used = [0]

        def part(words):
            used[0] += words
            return arena[:, used[0] - words:used[0]]

        xt = [part(HALVES * ROW).rearrange("p (a w) -> p a w", a=HALVES) for _ in range(4)]
        dsto = [part(HALVES).bitcast(I32) for _ in range(4)]
        dsti = [part(HALVES).bitcast(I32) for _ in range(4)]
        tabj = part(3 * TILES_B).rearrange("p (a j) -> p a j", a=3)
        yo = [part(HALVES * HID).rearrange("p (a h) -> p a h", a=HALVES) for _ in range(4)]
        xTs = [part(ROWS).bitcast(F16) for _ in range(2)]
        big, big2 = arena[:, used[0]:used[0] + TILES_B * E], arena[:, used[0] + TILES_B * E:used[0] + 2 * TILES_B * E]
        hf = [part(FC * ROWS) for _ in range(2)]
        hhi = [part(FC * ROWS // 2).bitcast(F16) for _ in range(4)]
        hlo = [part(FC * ROWS // 2).bitcast(F16) for _ in range(4)]
        bk = [patches[:, i, 0:2 * CT, :] for i in range(NX)]

        bank = [ctx.enter_context(nc.psum_tensor(f"bank{i}", [P, 512], F32)) for i in range(8)]
        ps_tok = bank[0:2]
        ps_gate = bank[2:4]
        ps_T, ps_h, ps_logit, ps_rank = bank[4:8]
        ps_down = bank[0:2]
        ps_in = [b[:, 0:ROWS].bitcast(F16) for b in bank[6:8]]

        def ps_up(n, c):
            b = bank[2 + 2 * n.mod(2) + c // 2]
            return b[:, c % 2 * ROWS:(c % 2 + 1) * ROWS]


        const_in = sem("const_in")
        w_in = sem("w_in")
        ones_in = sem("ones_in")
        setup_act = sem("setup_act")
        setup_dve = sem("setup_dve")
        setup_pool = sem("setup_pool")
        x_in = [sem(f"x_in{i}") for i in range(NX)]
        pos_in = [sem(f"pos_in{i}") for i in range(NPOS)]
        hi_done, lo_done, tok_done = sem("hi_done"), sem("lo_done"), sem("tok_done")
        h0_done, xn_done = sem("h0_done"), sem("xn_done")
        st1, st2, moments, veps_done, rstd_done = (sem(s) for s in ("st1", "st2", "moments", "veps_done", "rstd_done"))
        xT_ps, xT_done = sem("xT_ps"), sem("xT_done")
        gates_ps, gates_done = sem("gates_ps"), sem("gates_done")
        ca_done, cb_done, c_done, tc_done, h_done = sem("ca_done"), sem("cb_done"), sem("c_done"), sem("tc_done"), sem("h_done")
        h_ps, h1_done = sem("h_ps"), sem("h1_done")
        yn_done = sem("yn_done")
        pay_hi, pay_lo = sem("pay_hi"), sem("pay_lo")
        yT_ps, yT_done = sem("yT_ps"), sem("yT_done")
        logit_ps = sem("logit_ps")
        r_dve, r_exp, r_rank = sem("r_dve"), sem("r_exp"), sem("r_rank")
        slots_done, ids_done, sent_done = sem("slots_done"), sem("ids_done"), sem("sent_done")
        ex_in = [sem(f"ex_in{i}") for i in range(4)]
        ex_hi_done, ex_lo_done = sem("ex_hi_done"), sem("ex_lo_done")
        plan, plan_done = sem("plan"), sem("plan_done")
        pads_sp, pads_act = sem("pads_sp"), sem("pads_act")
        xt_in = [sem(f"xt_in{i}") for i in range(4)]
        b2_in = [sem(f"b2_in{i}") for i in range(4)]
        in_ps, in_done = sem("in_ps"), sem("in_done")
        up_ps, gelu_done, hhi_done, hlo_done = sem("up_ps"), sem("gelu_done"), sem("hhi_done"), sem("hlo_done")
        down_ps, y_done = sem("down_ps"), sem("y_done")
        dst_p, dst_a, dst_b = sem("dst_p"), sem("dst_a"), sem("dst_b")
        y_out = [sem(f"y_out{i}") for i in range(4)]
        bk_in = [sem(f"bk_in{i}") for i in range(NX)]
        add_a, add_b = sem("add_a"), sem("add_b")
        out_done = sem("out_done")

        N_CONST = 9
        R, R_MASK = 25, 18
        LAST_SLOT = T - 1 + 4

        def slots(eng, step, width, first, start, high, last):
            bodies = (high + 1 - start) // width
            for n in range(first, start):
                step(At(None, n, width))
            with eng.Fori(0, bodies) as i:
                for n in range(start, start + width):
                    step(At(i, n, width))
            for n in range(start + bodies * width, last + 1):
                step(At(None, n, width))

        def slots_a(eng, step, start, high, last=LAST_SLOT):
            slots(eng, step, U, -5, start, high, last)

        def slots_b(eng, step, start, high):
            slots(eng, step, UB, -3, start, high, TILES_B + 2)

        def group_at(n):
            if n.reg is None and n.at == 3:
                return At(None, 0, 1), At(None, 0, U), 1
            if n.at % U == 3 and n.at >= 11:
                return At(n.reg, n.at // U, 1), n - 10, U
            return None

        def through(eng, s, t):
            eng.wait_ge(s, (t + 1).val())

        def norms(n):
            there = [k for k, t in ((0, n + 2), (1, n - 1)) if t.within(0, T - 1)]
            return slice(there[0], there[-1] + 1) if there else None

        def normed(n):
            return (n + 3).val()

        def wait_alone(eng, s, v):
            v = v if isinstance(v, int) else eng.snap(v)
            eng.wait_ge(const_in, 16 * N_CONST)
            eng.wait_ge(s, v)

        def rows_of(region, row):
            return region[bass.ds(row, ROWS), :].rearrange("(p a) w -> p a w", a=HALVES)

        def patches_in(eng, t):
            eng.wait_ge(x_in[(t - 1).mod(NX)], ((t - 1).div(NX) + 1) * 32)

        block = ctx.enter_context(nc.Block())

        @block.sync
        def _(sp):
            for dst, src in ((cst[:, :], const),
                             (wih[:, :, :], w_ih), (whh[:, :, :], w_hh), (lbias[:, 0, :], b_ih),
                             (lbias[:, 1, :], b_hh), (rws[:, :], rw),
                             (rbs[:, :, :], rb.partition_broadcast(P)), (h0[:, 3, :], cls.partition_broadcast(P)),
                             (b1s[:, :], b1)):
                sp.dma_start(dst, src).then_inc(const_in, 16)

            def step(n):
                t = n + 6
                if t.within(1, T - 1):
                    if t.reg is None and t.at == 1:
                        sp.wait_ge(setup_dve, 1)
                    if t.reg is not None or t.at > NX:
                        sp.wait_ge(tok_done, (t - NX).val())
                        sp.wait_ge(lo_done, (t - NX).val())
                    q = (t - 1).mod(NX)
                    row = (t - 1).val() * IN_D
                    sp.dma_start(xraw[q][:, 0:KC, :],
                                 x[bass.ds(row, KC * P), :].rearrange("(p c) b -> p c b", c=KC)
                                 ).then_inc(x_in[q], 16)
                    sp.dma_start(xraw[q][0:KREST, KC, :], x[bass.ds(row + KC * P, KREST), :]
                                 ).then_inc(x_in[q], 16)
                t = n + 4
                if t.within(0, T - 1):
                    if t.reg is not None or t.at >= NPOS:
                        through(sp, h0_done, t - NPOS)
                    sp.dma_start(posr[:, t.mod(NPOS), :],
                                 pos[bass.ds(t.val(), 1), :].rearrange("a h -> (a h)").partition_broadcast(P)
                                 ).then_inc(pos_in[t.mod(NPOS)], 16)
                if n.within(0, PIECES - 1):
                    if n.reg is not None or n.at >= 4:
                        through(sp, ex_lo_done, n - 4)
                    sp.dma_start(ex_raw[:, n.mod(4), :], we[:, bass.ds(n.val() * PIECE, PIECE)]
                                 ).then_inc(ex_in[n.mod(4)], 16)

            slots_a(sp, step, 4, T - 7)

            sp.wait_ge(plan_done, 1)
            for e in range(0, E, 2):
                row = sp.value_load(padi[0:1, e:e + 1], min_val=0, max_val=E * CAP - ROWS)
                sp.dma_start(rows_of(sent, row), pad[:, :, :]).then_inc(pads_sp, 16)
            sp.wait_ge(sent_done, 32 * T)
            sp.wait_ge(pads_sp, 16 * E // 2)
            sp.wait_ge(pads_act, 16 * (E // 2 + 1))

            def step_b(n):
                j = n + 3
                if j.within(0, TILES_B - 1):
                    if j.reg is not None or j.at >= 4:
                        through(sp, in_ps, j - 4)
                        through(sp, dst_b, j - 4)
                    row = sp.value_load(tabi[0:1, 1, bass.ds(j.val(), 1)], min_val=0, max_val=E * CAP)
                    sp.dma_start(xt[j.mod(4)], rows_of(sent, row)).then_inc(xt_in[j.mod(4)], 16)
                j = n + 1
                if j.within(0, TILES_B - 1):
                    if j.reg is not None or j.at >= 4:
                        through(sp, y_done, j - 4)
                    e = sp.value_load(tabi[0:1, 0, bass.ds(j.val(), 1)], min_val=0, max_val=E - 1)
                    sp.dma_start(b2r[:, j.mod(4), :],
                                 b2[bass.ds(e, 1), :].rearrange("a h -> (a h)").partition_broadcast(P)
                                 ).then_inc(b2_in[j.mod(4)], 16)

            slots_b(sp, step_b, 3, TILES_B - 4)

            for q in range(4):
                sp.wait_ge(y_out[q], 16 * HALVES * len(range(q, TILES_B, 4)))
            steps = T // CT

            def load(m):
                q = m % NX
                if m >= NX:
                    sp.wait_ge(add_b, (m - NX + 1) * CT)
                for k in range(2):
                    sp.dma_start(bk[q][:, k * CT:(k + 1) * CT, :],
                                 back[k * TOKENS + m * CT * P:k * TOKENS + (m + 1) * CT * P, :].rearrange(
                                     "(t b) h -> b t h", b=P)).then_inc(bk_in[q], 16)

            for m in range(NX):
                load(m)
            for m in range(steps):
                sp.wait_ge(add_b, (m + 1) * CT)
                sp.dma_start(out[:, m * CT:(m + 1) * CT, :], h1[:, m * CT:(m + 1) * CT, :]).then_inc(out_done, 16)
                if m + NX < steps:
                    load(m + NX)
            sp.wait_ge(out_done, 16 * steps)

        @block.scalar
        def _(act):
            act.dma_start(ws[:, 0:KC, :], w).then_inc(w_in, 16)
            act.dma_start(ws[0:KBIAS + 1, KC, :], w_rest).then_inc(w_in, 16)
            act.wait_ge(w_in, 32)
            act.activation(whi[:, :, :], ws[:, 0:KS, :], ACT.Copy, scale=W_SCALE)
            act.activation(ws[:, KS:KC, :], ws[:, KS:KC, :], ACT.Copy, scale=W_SCALE)
            act.activation(ws[0:KBIAS + 1, KC, :], ws[0:KBIAS + 1, KC, :], ACT.Copy,
                           scale=W_SCALE).then_inc(setup_act, 1)
            act.wait_ge(const_in, 16 * N_CONST)
            act.activation(ident16[:, :], cst[:, C_ID:C_TRI], ACT.Copy)
            act.activation(tri16[:, :], cst[:, C_TRI:C_ONE], ACT.Copy)
            act.activation(ones16[:, :], cst[:, C_ONE:C_IOTA], ACT.Copy)
            act.activation(whh[:, :, :], whh[:, :, :], ACT.Copy, scale=0.5).then_inc(setup_act, 1)
            act.wait_ge(setup_dve, 4)

            def step(n):
                if n.within(0, T - 1):
                    through(act, gates_ps, n)
                    for g in range(4):
                        last = act.activation(gate[:, g, :], ps_gate[n.mod(2)][:, g * B:(g + 1) * B], ACT.Tanh,
                                              bias=lbias[:, 2, g:g + 1], scale=1.0 if g == 2 else 0.5)
                    last.then_inc(gates_done, 1)
                t = n - 2
                if t.within(0, T - 1):
                    through(act, yT_ps, t)
                    if t.reg is not None or t.at >= 2:
                        through(act, logit_ps, t - 2)
                    act.activation(ynT[:, t.mod(2), :], ps_T[:, P:2 * P], ACT.Copy).then_inc(yT_done, 1)
                t = n + 4
                split = t.within(1, T - 1)
                if split:
                    q, r = (t - 1).mod(NX), (t - 1).mod(2)
                    patches_in(act, t)
                    if t.reg is not None or t.at > 2:
                        act.wait_ge(tok_done, (t - 2).val())
                    act.activation(xhi[r][:, 0:KS // 2, :], xraw[q][:, 0:KS // 2, :], ACT.Copy)
                if n.within(0, T - 1):
                    through(act, c_done, n)
                    act.activation(tc[:, :], c2[:, :], ACT.Tanh, scale=0.5).then_inc(tc_done, 1)
                if split:
                    act.activation(xhi[r][:, KS // 2:KS, :], xraw[q][:, KS // 2:KS, :], ACT.Copy).then_inc(hi_done, 1)
                t = n + 2
                if t.within(0, T - 1):
                    through(act, xT_ps, t)
                    if t.reg is not None or t.at >= 2:
                        through(act, gates_ps, t - 2)
                    act.activation(xnT[:, t.mod(2), :], ps_T[:, 0:P], ACT.Copy).then_inc(xT_done, 1)
                if n.within(0, PIECES - 1):
                    act.wait_ge(ex_in[n.mod(4)], (n.div(4) + 1) * 16)
                    piece = ex_raw[:, n.mod(4), :]
                    flat_hi = ex_hi[:, :, :, :].rearrange("p e m f -> p (e m f)")
                    act.activation(flat_hi[:, bass.ds(n.val() * PIECE, PIECE)], piece, ACT.Copy, scale=E_SCALE)
                    act.activation(piece, piece, ACT.Copy, scale=E_SCALE).then_inc(ex_hi_done, 1)
                at = group_at(n)
                if at:
                    g, t0, m = at
                    act.wait_ge(r_dve, g.val() * R + 3)
                    act.activation(pr[:, 0:m, :], lg[:, 0:m, :], ACT.Exp).then_inc(r_exp, 1)

            slots_a(act, step, 5, T - 5)

            act.wait_ge(plan_done, 1)
            act.dma_start(rows_of(sent, E * CAP), pad[:, :, :]).then_inc(pads_act, 16)
            for e in range(1, E, 2):
                row = act.value_load(padi[0:1, e:e + 1], min_val=0, max_val=E * CAP - ROWS)
                act.dma_start(rows_of(sent, row), pad[:, :, :]).then_inc(pads_act, 16)

            def step_b(n):
                j = n + 1
                if j.within(0, TILES_B - 1):
                    through(act, in_ps, j)
                    if j.reg is not None or j.at >= 2:
                        through(act, up_ps, j - 2)
                    act.activation(xTs[j.mod(2)], ps_in[j.mod(2)], ACT.Copy).then_inc(in_done, 1)
                if n.within(0, TILES_B - 1):
                    e = act.value_load(tabi[0:1, 0, bass.ds(n.val(), 1)], min_val=0, max_val=E - 1)
                    through(act, up_ps, n)
                    if n.reg is not None or n.at >= 2:
                        through(act, hlo_done, n - 2)
                    for c in range(FC):
                        last = act.activation(hf[n.mod(2)][:, c * ROWS:(c + 1) * ROWS], ps_up(n, c), ACT.Gelu,
                                              bias=b1s[:, bass.ds(e * FC + c, 1)], scale=1.0 / E_SCALE)
                    last.then_inc(gelu_done, 1)

            slots_b(act, step_b, 2, TILES_B - 2)

        @block.vector
        def _(dve):
            for q in range(NX):
                dve.memset(xraw[q][KBIAS // 2:KBIAS, KC, :], 0.0)
                dve.memset(xraw[q][KBIAS:KBIAS + 1, KC, :], 1.0).then_inc(ones_in, 1)
            dve.wait_ge(ones_in, NX)
            dve.memset(c2[:, :], 0.0).then_inc(setup_dve, 1)
            dve.memset(slot[:, :, :], 0)
            dve.memset(h2[:, 1, :], 0.0)
            dve.wait_ge(setup_act, 1)
            dve.scalar_tensor_tensor(wlo[:, :, :].rearrange("p a b -> p (a b)"),
                                     ws[:, 0:KS, :].rearrange("p a b -> p (a b)"), W_SCALE,
                                     whi[:, :, :].rearrange("p a b -> p (a b)"), ALU.mult,
                                     ALU.subtract).then_inc(setup_dve, 1)
            dve.wait_ge(const_in, 16 * N_CONST)
            dve.tensor_copy(count[:, :], cst[:, C_EBASE:C_TOK])
            dve.tensor_tensor(lbias[:, 2, :], lbias[:, 0, :], lbias[:, 1, :], ALU.add).then_inc(setup_dve, 1)
            dve.wait_ge(setup_dve, 3)
            dve.tensor_tensor(lbias[:, 2, :], lbias[:, 2, :], cst[:, C_BSC:C_POW], ALU.mult).then_inc(setup_dve, 1)

            def scaled(t, k, src, dst, s_out):
                dve.tensor_scalar(dst, src, mv[:, k, 0:1], rstd[:, k:k + 1], ALU.subtract, ALU.mult).then_inc(s_out, 1)

            def step(n):
                if group_at(n):
                    route_logits(*group_at(n))
                t0, t1 = n + 2, n - 1
                pre, post = t0.within(0, T - 1), t1.within(0, T - 1)
                if pre:
                    src0 = h0[:, t0.mod(4), :]
                    dve.wait_ge(pos_in[t0.mod(NPOS)], (t0.div(NPOS) + 1) * 16)
                    if t0.reg is None and t0.at == 0:
                        dve.tensor_tensor(src0, h0[:, 3, :], posr[:, 0, :], ALU.mult).then_inc(h0_done, 1)
                    else:
                        dve.wait_ge(tok_done, t0.val())
                        dve.scalar_tensor_tensor(src0, ps_tok[t0.mod(2)][:, 0:HID], 1.0 / W_SCALE,
                                                 posr[:, t0.mod(NPOS), :], ALU.mult, ALU.mult).then_inc(h0_done, 1)
                if post:
                    through(dve, h_ps, t1)
                    src1 = h1[:, bass.ds(t1.val(), 1), :].rearrange("p a h -> p (a h)")
                    dve.scalar_tensor_tensor(src1, ps_h[:, 0:P], 0.5, h0[:, t1.mod(4), :], ALU.mult,
                                             ALU.add).then_inc(h1_done, 1)
                if pre:
                    wait_alone(dve, h0_done, (t0 + 1).val())
                    dve.bn_stats(stats[:, 0, :], src0).then_inc(st1, 1)
                if post:
                    wait_alone(dve, h1_done, (t1 + 1).val())
                    dve.bn_stats(stats[:, 1, :], src1).then_inc(st2, 1)
                if pre:
                    wait_alone(dve, st1, (t0 + 1).val())
                    ins = dve.bn_aggr(mv[:, 0, :], stats[:, 0, :])
                if post:
                    wait_alone(dve, st2, (t1 + 1).val())
                    ins = dve.bn_aggr(mv[:, 1, :], stats[:, 1, :])
                both = norms(n)
                if both:
                    ins.then_inc(moments, 1)
                    dve.wait_ge(moments, normed(n))
                    dve.tensor_scalar(veps[:, both], mv[:, both, 1], EPS, None, ALU.add).then_inc(veps_done, 1)
                if n.within(0, T - 1):
                    through(dve, gates_done, n)
                    dve.scalar_tensor_tensor(ca[:, :], gate[:, 1, :], 1.0, c2[:, :], ALU.add,
                                             ALU.mult).then_inc(ca_done, 1)
                    dve.scalar_tensor_tensor(cb[:, :], gate[:, 0, :], 1.0, gate[:, 2, :], ALU.add,
                                             ALU.mult).then_inc(cb_done, 1)
                    through(dve, cb_done, n)
                    through(dve, ca_done, n)
                    dve.scalar_tensor_tensor(c2[:, :], ca[:, :], 0.5, cb[:, :], ALU.mult, ALU.add).then_inc(c_done, 1)
                if both:
                    dve.wait_ge(rstd_done, normed(n))
                if pre:
                    if t0.reg is not None or t0.at >= 2:
                        through(dve, xT_ps, t0 - 2)
                    scaled(t0, 0, src0, xn[:, t0.mod(2), :], xn_done)
                if post:
                    if t1.reg is not None or t1.at >= NY:
                        through(dve, pay_lo, t1 - NY)
                        through(dve, yT_ps, t1 - NY)
                    scaled(t1, 1, src1, yn[:, t1.mod(NY), :], yn_done)
                if n.within(0, T - 1):
                    through(dve, tc_done, n)
                    dve.scalar_tensor_tensor(h2[:, n.mod(2), :], gate[:, 3, :], 1.0, tc[:, :], ALU.add,
                                             ALU.mult).then_inc(h_done, 1)
                t = n + 4
                if t.within(1, T - 1):
                    q, r = (t - 1).mod(NX), (t - 1).mod(2)
                    dve.wait_ge(hi_done, t.val())
                    dve.tensor_tensor(xlo[r][:, :, :], xraw[q][:, 0:KS, :], xhi[r][:, :, :],
                                      ALU.subtract).then_inc(lo_done, 1)
                if group_at(n):
                    route_masks(*group_at(n))
                if group_at(n - 1):
                    route_slots(*group_at(n - 1))

            def route_logits(g, t0, m):
                dve.wait_ge(logit_ps, (t0 + m).val())
                if g.reg is not None or g.at >= 1:
                    dve.wait_ge(r_dve, g.val() * R)
                dve.tensor_tensor(lg[:, 0:m, :], ps_logit[:, 0:m * E].rearrange("p (t e) -> p t e", e=E),
                                  rbs[:, 0:m, :], ALU.add).then_inc(r_dve, 1)

            def route_masks(g, t0, m):
                count_of = [1]

                def by(ins):
                    ins.then_inc(r_dve, 1)
                    count_of[0] += 1

                def seen():
                    dve.wait_ge(r_dve, g.val() * R + count_of[0])

                def wide(row):
                    return row.unsqueeze(2).to_broadcast([P, m, E])

                def lines(a):
                    return a.rearrange("p t e -> p (t e)")

                L, Q, Q2, K = (a[:, 0:m, :] for a in (lg, pr, pr2, cand))
                OH = [oh[:, k, 0:m, :] for k in range(2)]
                iota = cst[:, C_IOTA:C_IOTA + m * E].rearrange("p (t e) -> p t e", e=E)
                most = [gates[:, k, bass.ds(t0.val(), m)] for k in range(2)]
                first_of = first[:, bass.ds(t0.val(), m)]
                seen()
                by(dve.tensor_reduce(red[:, 0, 0:m], L, AX.X, ALU.max))
                seen()
                by(dve.tensor_tensor(L, L, wide(red[:, 0, 0:m]), ALU.subtract))
                dve.wait_ge(r_exp, (g + 1).val())
                by(dve.tensor_reduce(red[:, 1, 0:m], Q, AX.X, ALU.add))
                seen()
                by(dve.reciprocal(red[:, 2, 0:m], red[:, 1, 0:m]))
                seen()
                by(dve.tensor_tensor(Q, Q, wide(red[:, 2, 0:m]), ALU.mult))
                seen()
                which = (first_of, red[:, 3, 0:m])
                for k, q in enumerate((Q, Q2)):
                    by(dve.tensor_reduce(most[k], q, AX.X, ALU.max))
                    seen()
                    by(dve.tensor_tensor(L, q, wide(most[k]), ALU.is_lt))
                    seen()
                    by(dve.scalar_tensor_tensor(lines(K), lines(L), float(E), lines(iota), ALU.mult, ALU.add))
                    seen()
                    by(dve.tensor_reduce(which[k], K, AX.X, ALU.min))
                    seen()
                    by(dve.tensor_tensor(OH[k], iota, wide(which[k]), ALU.is_equal))
                    seen()
                    if k == 0:
                        by(dve.scalar_tensor_tensor(lines(Q2), lines(OH[0]), -2.0, lines(Q), ALU.mult, ALU.add))
                        seen()
                by(dve.tensor_tensor(mask16[:, 0:m, :], OH[0], OH[1], ALU.add))
                assert count_of[0] == R_MASK

            def route_slots(g, t0, m):
                count_of = [R_MASK]

                def by(ins):
                    ins.then_inc(r_dve, 1)
                    count_of[0] += 1

                def seen():
                    dve.wait_ge(r_dve, g.val() * R + count_of[0])

                K, Q2 = cand[:, 0:m, :], pr2[:, 0:m, :]
                OH = [oh[:, k, 0:m, :] for k in range(2)]
                dve.wait_ge(r_rank, (g + 1).val())
                by(dve.tensor_tensor(rank[:, 0:m, :], ps_rank[:, 0:m * E].rearrange("p (t e) -> p t e", e=E),
                                     count[:, :].unsqueeze(1).to_broadcast([P, m, E]), ALU.add))
                seen()
                by(dve.tensor_tensor(count[:, :], count[:, :], ps_rank[:, P:P + E], ALU.add))
                seen()
                by(dve.tensor_tensor(K, rank[:, 0:m, :], OH[0], ALU.mult))
                by(dve.tensor_tensor(Q2, rank[:, 0:m, :], OH[1], ALU.mult))
                seen()
                by(dve.tensor_reduce(slotf[:, 0, 0:m], K, AX.X, ALU.add))
                by(dve.tensor_reduce(slotf[:, 1, 0:m], Q2, AX.X, ALU.add))
                seen()
                if g.reg is not None or g.at >= 1:
                    dve.wait_ge(ids_done, g.val())
                by(dve.tensor_copy(slot[:, :, 0:m], slotf[:, :, 0:m]))
                assert count_of[0] == R

            slots_a(dve, step, 1 + NY, T - 5)

            done = [0]

            def by(ins):
                ins.then_inc(plan, 1)
                done[0] += 1

            def seen():
                dve.wait_ge(plan, done[0])

            dve.wait_ge(r_dve, R * (1 + (T - 1) // U))
            by(dve.tensor_copy(padi[:, :], count[0:1, :]))
            by(dve.tensor_tensor(tabs[:, 0, :], count[:, :], cst[:, C_EBASE:C_TOK], ALU.subtract))
            by(dve.memset(pad[:, :, :], 0.0))
            seen()
            by(dve.memset(pad[:, :, HID:HID + 1].bitcast(I32), NO_TOKEN))
            whole = [tabs[:, k, :].bitcast(I32) for k in (1, 2)]
            by(dve.tensor_scalar(whole[0], tabs[:, 0, :], float(ROWS - 1), None, ALU.add))
            seen()
            by(dve.tensor_scalar(whole[1], whole[0], ROWS.bit_length() - 1, ROWS.bit_length() - 1, ALU.logical_shift_right, ALU.logical_shift_left))
            seen()
            by(dve.tensor_copy(tabs[:, 3, :], whole[1]))
            seen()
            length, row = tabs[:, 3, :], 3
            for k in (1, 2, 4, 8):
                by(dve.tensor_tensor(tabs[:, row + 1, k:E], tabs[:, row, k:E], tabs[:, row, 0:E - k], ALU.add))
                by(dve.tensor_copy(tabs[:, row + 1, 0:k], tabs[:, row, 0:k]))
                seen()
                row += 1
            ends = tabs[:, row, :]
            start_j = cst[:, C_J:C_END]
            over = big.rearrange("p (j e) -> p j e", e=E)
            over2 = big2.rearrange("p (j e) -> p j e", e=E)
            by(dve.tensor_tensor(over, start_j.unsqueeze(2).to_broadcast([P, TILES_B, E]),
                                 ends.unsqueeze(1).to_broadcast([P, TILES_B, E]), ALU.is_ge))
            seen()
            by(dve.tensor_reduce(tabj[:, 0, :], over, AX.X, ALU.add))
            by(dve.tensor_tensor(over2, over, length.unsqueeze(1).to_broadcast([P, TILES_B, E]), ALU.mult))
            seen()
            by(dve.tensor_reduce(tabj[:, 1, :], over2, AX.X, ALU.add))
            by(dve.tensor_scalar(tabj[:, 2, :], tabj[:, 0, :], float(CAP), None, ALU.mult))
            seen()
            by(dve.tensor_tensor(tabj[:, 1, :], start_j, tabj[:, 1, :], ALU.subtract))
            by(dve.tensor_scalar(tabj[:, 0, :], tabj[:, 0, :], float(E - 1), None, ALU.min))
            seen()
            by(dve.tensor_tensor(tabj[:, 1, :], tabj[:, 1, :], tabj[:, 2, :], ALU.add))
            by(dve.tensor_copy(tabi[:, 0, :], tabj[0:1, 0, :]))
            seen()
            dve.tensor_scalar(tabi[:, 1, :], tabj[0:1, 1, :], float(E * CAP), None, ALU.min).then_inc(plan_done, 1)

            def step_b(n):
                if n.within(0, TILES_B - 1):
                    q = n.mod(4)
                    dve.wait_ge(xt_in[q], (n.div(4) + 1) * 16)
                    if n.reg is not None or n.at >= 4:
                        dve.wait_ge(y_out[q], n.div(4) * 16 * HALVES)
                    dve.tensor_scalar(dsto[q], xt[q][:, :, HID + 1], tabj[:, 0, bass.ds(n.val(), 1)],
                                      float(TOKENS), ALU.not_equal, ALU.mult).then_inc(dst_a, 1)
                j = n - 2
                if j.within(0, TILES_B - 1):
                    q = j.mod(4)
                    through(dve, down_ps, j)
                    dve.wait_ge(b2_in[q], (j.div(4) + 1) * 16)
                    dve.scalar_tensor_tensor(yo[q], ps_down[j.mod(2)][:, 0:HALVES * HID].rearrange(
                                                 "p (a h) -> p a h", a=HALVES), 1.0 / E_SCALE,
                                             b2r[:, q, :].unsqueeze(1).to_broadcast([P, HALVES, HID]), ALU.mult,
                                             ALU.add).then_inc(y_done, 1)
                if n.within(0, TILES_B - 1):
                    through(dve, gelu_done, n)
                    if n.reg is not None or n.at >= 4:
                        through(dve, down_ps, n - 4)
                    dve.tensor_copy(hhi[n.mod(4)], hf[n.mod(2)]).then_inc(hhi_done, 1)
                    through(dve, hhi_done, n)
                    dve.tensor_tensor(hlo[n.mod(4)], hf[n.mod(2)], hhi[n.mod(4)], ALU.subtract).then_inc(hlo_done, 1)

            slots_b(dve, step_b, 6, TILES_B - 1)

            for m in range(T // CT):
                q = m % NX
                dve.wait_ge(bk_in[q], 32 * (m // NX + 1))
                for k, s in ((0, add_a), (1, add_b)):
                    for i in range(CT):
                        t = m * CT + i
                        if k == 1:
                            dve.wait_ge(add_a, t + 1)
                        dve.scalar_tensor_tensor(h1[:, t, :], bk[q][:, k * CT + i, :], gates[:, k, t:t + 1],
                                                 h1[:, t, :], ALU.mult, ALU.add).then_inc(s, 1)

        @block.gpsimd
        def _(pool):
            pool.wait_ge(const_in, 16 * N_CONST)

            def step(n):
                sent_t = n - 12
                sends = sent_t.within(0, T - 1)
                if sends:
                    if sent_t.reg is None and sent_t.at == 0:
                        g, col = At(None, 0, 1), 0
                    else:
                        g, col = At(sent_t.reg, (sent_t.at - 1) // U + 1, 1), (sent_t.at - 1) % U
                    if col == 0:
                        pool.wait_ge(r_dve, (g.val() + 1) * R)
                        if sent_t.reg is not None or sent_t.at >= 1:
                            pool.wait_ge(sent_done, sent_t.val() * 32)
                both = norms(n)
                if both:
                    pool.wait_ge(veps_done, normed(n))
                    pool.tensor_tensor(rstd[:, both], veps[:, both],
                                       cst[:, C_POW:C_POW + 1].to_broadcast([P, both.stop - both.start]),
                                       ALU.pow).then_inc(rstd_done, 1)
                if sends:
                    if col == 0:
                        pool.tensor_copy(slot_own[:, :, :], slot[:, :, :]).then_inc(ids_done, 1)
                    pool.tensor_copy(pay[:, sent_t.mod(NY), HID + 1:HID + 2],
                                     first[:, bass.ds(sent_t.val(), 1)]).then_inc(dst_p, 1)
                    pool.wait_ge(ids_done, (g + 1).val())
                    through(pool, dst_p, sent_t)
                    through(pool, pay_lo, sent_t)
                t = n - 5
                packs = t.within(0, T - 1)
                if packs:
                    through(pool, yn_done, t)
                    if t.reg is not None or t.at >= NY:
                        pool.wait_ge(sent_done, (t - NY + 1).val() * 32)
                piece = n - 1
                if piece.within(0, PIECES - 1):
                    through(pool, ex_hi_done, piece)
                    flat_hi = ex_hi[:, :, :, :].rearrange("p e m f -> p (e m f)")
                    flat_lo = ex_lo[:, :, :, :].rearrange("p e m f -> p (e m f)")
                    here = bass.ds(piece.val() * PIECE, PIECE)
                    pool.tensor_tensor(flat_lo[:, here], ex_raw[:, piece.mod(4), :], flat_hi[:, here],
                                       ALU.subtract).then_inc(ex_lo_done, 1)
                if sends:
                    for k in range(2):
                        pool.indirect_dma_start(
                            sent, bass.IndirectOffsetOnAxis(ap=slot_own[:, k, col:col + 1], axis=0),
                            pay[:, sent_t.mod(NY), :], None, bounds_check=E * CAP - 1, oob_is_err=False
                        ).then_inc(sent_done, 16)
                if packs:
                    q = t.mod(NY)
                    halves = pay[:, q, 0:HID].bitcast(F16)
                    pool.tensor_copy(halves[:, 0:HID], yn[:, q, :]).then_inc(pay_hi, 1)
                    pool.tensor_copy(pay[:, q, HID:HID + 1].bitcast(I32), cst[:, bass.ds(t.val() + C_TOK, 1)])
                    through(pool, pay_hi, t)
                    pool.tensor_tensor(halves[:, HID:2 * HID], yn[:, q, :], halves[:, 0:HID],
                                       ALU.subtract).then_inc(pay_lo, 1)

            slots_a(pool, step, 13, PIECES - 1, T - 1 + 12)

            def step_b(n):
                j = n - 2
                sends = j.within(0, TILES_B - 1)
                if sends:
                    through(pool, dst_b, j)
                    through(pool, y_done, j)
                if n.within(0, TILES_B - 1):
                    through(pool, dst_a, n)
                    q = n.mod(4)
                    pool.tensor_tensor(dsti[q], dsto[q], xt[q][:, :, HID].bitcast(I32), ALU.add).then_inc(dst_b, 1)
                if sends:
                    q = j.mod(4)
                    for k in range(HALVES):
                        pool.indirect_dma_start(back, bass.IndirectOffsetOnAxis(ap=dsti[q][:, k:k + 1], axis=0),
                                                yo[q][:, k, :], None, bounds_check=2 * TOKENS - 1,
                                                oob_is_err=False).then_inc(y_out[q], 16)

            pool.wait_ge(plan_done, 1)
            slots_b(pool, step_b, 6, TILES_B - 1)

        @block.tensor
        def _(pe):
            pe.wait_ge(setup_act, 2)
            pe.wait_ge(setup_dve, 4)
            ident = cst[:, C_ID:C_TRI]

            def project(t, a, b):
                bank_of, q, r = ps_tok[t.mod(2)][:, 0:HID], (t - 1).mod(NX), (t - 1).mod(2)
                for c in range(a, b):
                    if c < KS:
                        parts = [(l[r][:, c, :], w_[:, c, :]) for l, w_ in ((xhi, whi), (xhi, wlo), (xlo, whi))]
                    else:
                        rows = slice(0, P if c < KC else KBIAS + 1)
                        parts = [(xraw[q][rows, c, :], ws[rows, c, :])]
                    for k, (l, w_) in enumerate(parts):
                        last = pe.matmul(bank_of, l, w_, start=(c == KS and k == 0), stop=(c == KS - 1 and k == 2))
                return last

            def step(n):
                if n.within(0, T - 1):
                    if n.reg is not None or n.at >= 1:
                        through(pe, h_done, n - 1)
                    for g in range(4):
                        last = pe.matmul(ps_gate[n.mod(2)][:, g * B:(g + 1) * B], whh[:, g, :],
                                         h2[:, (n - 1).mod(2), :], start=False, stop=True, skip_group_check=True)
                    last.then_inc(gates_ps, 1)
                t = n - 1
                if t.within(0, T - 1):
                    through(pe, h_done, t)
                    if t.reg is not None or t.at >= 1:
                        through(pe, h1_done, t - 1)
                    pe.transpose(ps_h[:, 0:P], h2[:, t.mod(2), :], ident).then_inc(h_ps, 1)
                t = n - 2
                if t.within(0, T - 1):
                    through(pe, yn_done, t)
                    if (t + 3).within(0, T - 1):
                        through(pe, xT_done, t + 3)
                    if t.reg is not None or t.at >= 1:
                        through(pe, yT_done, t - 1)
                    pe.transpose(ps_T[:, P:2 * P], yn[:, t.mod(NY), :], ident).then_inc(yT_ps, 1)
                t = n + 1
                if t.within(0, T - 1):
                    through(pe, xT_done, t)
                    if t.reg is not None or t.at >= 2:
                        through(pe, gates_done, t - 2)
                    for g in range(4):
                        pe.matmul(ps_gate[t.mod(2)][:, g * B:(g + 1) * B], wih[:, g, :], xnT[:, t.mod(2), :],
                                  start=(g == 0), stop=False, skip_group_check=True)
                t = n + 3
                proj = t.within(1, T - 1)
                if proj:
                    patches_in(pe, t)
                    if t.reg is not None or t.at > 2:
                        through(pe, h0_done, t - 2)
                    project(t, KS, KC + 1)
                t = n + 2
                if t.within(0, T - 1):
                    through(pe, xn_done, t)
                    if t.reg is not None or t.at >= 4:
                        through(pe, yT_done, t - 4)
                    pe.transpose(ps_T[:, 0:P], xn[:, t.mod(2), :], ident).then_inc(xT_ps, 1)
                at = group_at(n - 1)
                if at:
                    g, t0, m = at
                    pe.wait_ge(r_dve, g.val() * R + R_MASK)
                    pe.matmul(ps_rank[:, 0:m * E], tri16[:, :], mask16[:, 0:m, :], start=True, stop=False,
                              skip_group_check=True)
                    for k in range(1, m):
                        pe.matmul(ps_rank[:, k * E:m * E], ones16[:, :], mask16[:, 0:m - k, :], start=False,
                                  stop=False, skip_group_check=True)
                    for k in range(m):
                        last = pe.matmul(ps_rank[:, P:P + E], ones16[:, :], mask16[:, k, :], start=False,
                                         stop=True, skip_group_check=True)
                    last.then_inc(r_rank, 1)
                if proj:
                    pe.wait_ge(lo_done, (n + 3).val())
                    project(n + 3, 0, KS).then_inc(tok_done, 1)
                t = n - 2
                if t.within(0, T - 1):
                    through(pe, yT_done, t)
                    if t.reg is None and t.at == 0:
                        col = 0
                    else:
                        col = (t.at - 1) % U
                        if col == 0:
                            g = At(t.reg, (t.at - 1) // U, 1)
                            pe.wait_ge(r_dve, g.val() * R + 1)
                    pe.matmul(ps_logit[:, col * E:(col + 1) * E], ynT[:, t.mod(2), :], rws[:, :], start=True,
                              stop=True).then_inc(logit_ps, 1)
            slots_a(pe, step, 5, T - 4)
            pe.wait_ge(plan_done, 1)
            pe.wait_ge(ex_lo_done, PIECES)
            pe.wait_ge(gates_done, T)
            pe.wait_ge(yT_done, T)

            def step_b(n):
                j = n + 1
                if j.within(0, TILES_B - 1):
                    pe.wait_ge(xt_in[j.mod(4)], (j.div(4) + 1) * 16)
                    if j.reg is not None or j.at >= 2:
                        through(pe, in_done, j - 2)
                    for a in range(HALVES):
                        parts = xt[j.mod(4)][:, a, 0:HID].bitcast(F16)
                        for k in range(2):
                            last = pe.transpose(ps_in[j.mod(2)][:, k * ROWS + a * P:k * ROWS + (a + 1) * P],
                                                parts[:, k * P:(k + 1) * P], ident16[:, :])
                    last.then_inc(in_ps, 1)
                if n.within(0, TILES_B - 1):
                    e = pe.value_load(tabi[0:1, 0, bass.ds(n.val(), 1)], min_val=0, max_val=E - 1)
                    through(pe, in_done, n)
                    if n.reg is not None or n.at >= 2:
                        through(pe, gelu_done, n - 2)
                    x_hi, x_lo = xTs[n.mod(2)][:, 0:ROWS], xTs[n.mod(2)][:, ROWS:2 * ROWS]
                    for c in range(FC):
                        for k, (w_, r) in enumerate(((ex_hi, x_hi), (ex_hi, x_lo), (ex_lo, x_hi))):
                            w1 = w_[:, bass.ds(e, 1), 0, c * P:(c + 1) * P].rearrange("p a f -> p (a f)")
                            last = pe.matmul(ps_up(n, c), w1, r, start=(k == 0), stop=(k == 2))
                    last.then_inc(up_ps, 1)
                j = n - 2
                if j.within(0, TILES_B - 1):
                    e = pe.value_load(tabi[0:1, 0, bass.ds(j.val(), 1)], min_val=0, max_val=E - 1)
                    through(pe, hlo_done, j)
                    if j.reg is not None or j.at >= 2:
                        through(pe, y_done, j - 2)
                    for c in range(FC):
                        for k, (h_, w_) in enumerate(((hhi, ex_hi), (hlo, ex_hi), (hhi, ex_lo))):
                            w2 = w_[:, bass.ds(e, 1), 1, c * HID:(c + 1) * HID].rearrange("p a f -> p (a f)")
                            for a in range(HALVES):
                                h = h_[j.mod(4)][:, c * ROWS + a * P:c * ROWS + (a + 1) * P]
                                last = pe.matmul(ps_down[j.mod(2)][:, a * HID:(a + 1) * HID], h, w2,
                                                 start=(c == 0 and k == 0 and a == 0), stop=(c == FC - 1 and k == 2),
                                                 skip_group_check=True)
                    last.then_inc(down_ps, 1)

            slots_b(pe, step_b, 4, TILES_B - 2)


def kernel(**inputs):
    import concourse.bacc as bacc
    from concourse.bass_utils import run_bass_kernel_spmd as run

    a = {k: np.asarray(v) for k, v in inputs.items()}

    def whole(v):
        return np.ascontiguousarray(v)

    x = a["x"].reshape(B, C, GRID, PATCH, GRID, PATCH).transpose(2, 4, 1, 3, 5, 0)
    w = a["L0_tok_W"].T
    w1 = a["L0_ffn_w1"].transpose(2, 0, 1)
    w2 = a["L0_ffn_w2"].reshape(E, HID, FC, P).transpose(3, 0, 2, 1)
    arrays = {
        "x": whole(x).reshape((T - 1) * IN_D, B),
        "w": whole(w[:KC * P]).reshape(P, KC, HID),
        "w_rest": whole(np.concatenate([w[KC * P:], np.zeros((KBIAS - KREST, HID), np.float32),
                                        a["L0_tok_b"].reshape(1, HID)])),
        "cls": whole(a["L0_tok_class_token"]).reshape(HID),
        "pos": whole(a["L0_tok_pos_embed"]),
        "w_ih": whole(a["L0_attn_W_ih"].reshape(4, HID, HID).transpose(2, 0, 1)),
        "w_hh": whole(a["L0_attn_W_hh"].reshape(4, HID, HID).transpose(2, 0, 1)),
        "b_ih": whole(a["L0_attn_b_ih"].reshape(4, HID).T),
        "b_hh": whole(a["L0_attn_b_hh"].reshape(4, HID).T),
        "rw": whole(a["L0_ffn_router_w"].T),
        "rb": whole(np.broadcast_to(a["L0_ffn_router_b"], (U, E))),
        "we": whole(np.stack([w1, w2.reshape(P, E, FC * HID)], axis=2)).reshape(P, E * 2 * FF),
        "b1": whole(a["L0_ffn_b1"].reshape(E, FC, P).transpose(2, 0, 1)).reshape(P, E * FC),
        "b2": whole(a["L0_ffn_b2"]),
        "const": constants(),
    }
    nc = bacc.Bacc("TRN2", target_bir_lowering=False, num_devices=1)
    args = {k: nc.dram_tensor(f"in_{k}", list(v.shape), mybir.dt.from_np(v.dtype), kind="ExternalInput").ap()
            for k, v in arrays.items()}
    out = nc.dram_tensor("out_tower", [B, T, HID], mybir.dt.float32, kind="ExternalOutput").ap()
    tower(nc, out=out, **args)
    r = run(nc, [{f"in_{k}": v for k, v in arrays.items()}], core_ids=[0])
    return r.results[0]["out_tower"]
```

```python
from contextlib import ExitStack

import numpy as np

import concourse.bass as bass
from concourse import mybir

P = 128
B, C, IMG, GRID, HID = 128, 3, 224, 8, 128
PATCH = IMG // GRID
IN_D = C * PATCH * PATCH
T = GRID * GRID + 1
KC = IN_D // P
KREST = IN_D - KC * P
KBIAS = 64
KS = 8
E, FF = 16, 512
FC = FF // P
TOKENS = T * B
HALVES = 2
ROWS = HALVES * P
CAP = TOKENS + ROWS
TILES_B = (2 * TOKENS - E) // ROWS + E
ROW = HID + 2
EPS = 1e-5
W_SCALE = 1024.0
G_SCALE = 256.0
E_SCALE = 256.0
PIECE = 256
PIECES = E * 2 * FF // PIECE
U = 8
UG = 4
GROUPS = 1 + (T - 1) // UG
UB = 8
NX = 4
NPOS = 4
NY = 8
PACK, SEND = 5, 10
NO_TOKEN = 1 << 20
CT = 5

C_ID, C_TRI, C_ONE, C_IOTA, C_EBASE, C_TOK, C_BSC, C_POW, C_J = np.cumsum([0, P, P, P, UG * E, E, T, 4, 1]).tolist()
C_END = C_J + 1


def constants():
    c = np.zeros((P, C_END), np.float32)
    c[:, C_ID:C_TRI] = np.eye(P)
    c[:, C_TRI:C_ONE] = np.triu(np.ones((P, P)), 1)
    c[:, C_ONE:C_IOTA] = 1.0
    c[:, C_IOTA:C_EBASE] = np.tile(np.arange(E), UG)
    c[:, C_EBASE:C_TOK] = np.arange(E) * CAP
    c[:, C_TOK:C_BSC] = T * np.arange(P)[:, None] + np.arange(T)
    c[:, C_POW] = -0.5
    c[:, C_BSC:C_POW] = [0.5, 0.5, 1.0, 0.5]
    c[:, C_J] = ROWS * np.arange(P)
    return c


class At:

    def __init__(self, reg, at, width):
        self.reg, self.at, self.width = reg, at, width

    def __add__(self, k):
        return At(self.reg, self.at + k, self.width)

    def __sub__(self, k):
        return self + -k

    def within(self, low, high):
        return self.reg is not None or low <= self.at <= high

    def val(self):
        return self.at if self.reg is None else self.reg * self.width + self.at

    def mod(self, m):
        assert self.width % m == 0 or self.reg is None
        return self.at % m

    def div(self, m):
        assert self.width % m == 0 or self.reg is None
        return self.at // m if self.reg is None else self.reg * (self.width // m) + self.at // m


def tower(nc, x, w, w_rest, cls, pos, w_ih, w_hh, b_ih, b_hh, rw, rb, we, b1, b2, const, out):
    F32, F16, I32 = mybir.dt.float32, mybir.dt.float16, mybir.dt.int32
    ALU, ACT, AX = mybir.AluOpType, mybir.ActivationFunctionType, mybir.AxisListType
    ctx = ExitStack()
    with ctx:
        def sb(name, shape, dt=F32):
            return ctx.enter_context(nc.sbuf_tensor(name, shape, dt))

        def sem(name):
            return ctx.enter_context(nc.semaphore(name))

        sent = nc.dram_tensor("sent", [E * CAP + ROWS, ROW], F32, kind="Internal").ap()
        back = nc.dram_tensor("back", [2 * TOKENS, HID], F32, kind="Internal").ap()

        cst = sb("cst", [P, C_END])
        ident16 = sb("ident16", [P, P], F16)
        tri16 = sb("tri16", [P, P], F16)
        ones16 = sb("ones16", [P, P], F16)
        patches = sb("patches", [P, NX, KC + 1, P])
        xraw = [patches[:, i] for i in range(NX)]
        xhi = [sb(f"xhi{i}", [P, KS, P], F16) for i in range(2)]
        xlo = [sb(f"xlo{i}", [P, KS, P], F16) for i in range(2)]
        ws = sb("ws", [P, KC + 1, HID])
        whi = sb("whi", [P, KS, HID], F16)
        wlo = sb("wlo", [P, KS, HID], F16)
        posr = sb("posr", [P, NPOS, HID])
        wih = sb("wih", [HID, 4, HID])
        whh = sb("whh", [HID, 4, HID])
        lbias = sb("lbias", [HID, 3, 4])
        rws = sb("rws", [HID, E])
        rbs = sb("rbs", [P, UG, E])
        ex_hi = sb("ex_hi", [P, E, 2, FF], F16)
        ex_lo = sb("ex_lo", [P, E, 2, FF], F16)
        ex_raw = sb("ex_raw", [P, 4, PIECE])
        b1s = sb("b1s", [P, E * FC])
        b2r = sb("b2r", [P, 4, HID])
        h0 = sb("h0", [P, 4, HID])
        stats = sb("stats", [P, 2, 6])
        mv = sb("mv", [P, 2, 2])
        veps = sb("veps", [P, 2])
        rstd = sb("rstd", [P, 2])
        xn = sb("xn", [P, 2, HID])
        xT_hi = sb("xT_hi", [HID, 2, B], F16)
        xT_lo = sb("xT_lo", [HID, 2, B], F16)
        wih_hi = sb("wih_hi", [HID, 4, HID], F16)
        wih_lo = sb("wih_lo", [HID, 4, HID], F16)
        gate = sb("gate", [HID, 4, B])
        c2 = sb("c2", [HID, B])
        ca = sb("ca", [HID, B])
        cb = sb("cb", [HID, B])
        tc = sb("tc", [HID, B])
        h2 = sb("h2", [HID, 2, B])
        h1 = sb("h1", [P, T, HID])
        yn = sb("yn", [P, NY, HID])
        ynT = sb("ynT", [HID, 2, B])
        pay = sb("pay", [P, NY, ROW])
        lg = sb("lg", [P, UG, E])
        pr = sb("pr", [P, UG, E])
        pr2 = sb("pr2", [P, UG, E])
        cand = sb("cand", [P, UG, E])
        oh = sb("oh", [P, 2, UG, E])
        mask16 = sb("mask16", [P, UG, E], F16)
        rank = sb("rank", [P, UG, E])
        red = sb("red", [P, 4, UG])
        gates = sb("gates", [P, 2, T])
        tag = sb("tag", [P, T, 2])
        count = sb("count", [P, E])
        slotf = sb("slotf", [P, 2, UG])
        slot = sb("slot", [P, 2, UG], I32)
        slot_own = sb("slot_own", [P, 2, 2, UG], I32)
        tabs = sb("tabs", [P, 10, E])
        tab1 = sb("tab1", [P, 3])
        diagonals = sb("diagonals", [P, 2, TILES_B])
        tabi = sb("tabi", [1, 2, TILES_B], I32)
        padi = sb("padi", [1, E], I32)
        pad = sb("pad", [P, HALVES, ROW])

        arena = patches[:, :, :, :].rearrange("p q c b -> p (q c b)")
        used = [0]

        def part(words):
            used[0] += words
            return arena[:, used[0] - words:used[0]]

        xt = [part(HALVES * ROW).rearrange("p (a w) -> p a w", a=HALVES) for _ in range(4)]
        dsto = [part(HALVES).bitcast(I32) for _ in range(4)]
        dsti = [part(HALVES).bitcast(I32) for _ in range(4)]
        tabj = part(2 * TILES_B).rearrange("p (a j) -> p a j", a=2)
        yo = [part(HALVES * HID).rearrange("p (a h) -> p a h", a=HALVES) for _ in range(4)]
        xTs = [part(ROWS).bitcast(F16) for _ in range(2)]
        hf = [part(FC * ROWS) for _ in range(2)]
        hhi = [part(FC * ROWS // 2).bitcast(F16) for _ in range(4)]
        hlo = [part(FC * ROWS // 2).bitcast(F16) for _ in range(4)]
        bk = [patches[:, i, 0:2 * CT, :] for i in range(NX)]

        bank = [ctx.enter_context(nc.psum_tensor(f"bank{i}", [P, 512], F32)) for i in range(8)]
        ps_tok = bank[0:2]
        ps_gate = bank[2:4]
        ps_T, ps_h, ps_logit, ps_rank = bank[4:8]
        ps_down = bank[0:2]
        ps_in = [b[:, 0:ROWS].bitcast(F16) for b in bank[6:8]]

        def ps_up(n, c):
            b = bank[2 + 2 * n.mod(2) + c // 2]
            return b[:, c % 2 * ROWS:(c % 2 + 1) * ROWS]

        const_in = sem("const_in")
        w_in = sem("w_in")
        ones_in = sem("ones_in")
        setup_act = sem("setup_act")
        setup_dve = sem("setup_dve")
        x_in = [sem(f"x_in{i}") for i in range(NX)]
        pos_in = [sem(f"pos_in{i}") for i in range(NPOS)]
        hi_done, lo_done, tok_done = sem("hi_done"), sem("lo_done"), sem("tok_done")
        h0_done, xn_done = sem("h0_done"), sem("xn_done")
        st1, st2, moments = sem("st1"), sem("st2"), sem("moments")
        veps_done, rstd_done = sem("veps_done"), sem("rstd_done")
        xT_ps, xT_hi_done, xT_lo_done = sem("xT_ps"), sem("xT_hi_done"), sem("xT_lo_done")
        gates_ps, gates_done = sem("gates_ps"), sem("gates_done")
        ca_done, cb_done, c_done = sem("ca_done"), sem("cb_done"), sem("c_done")
        tc_done, h_done = sem("tc_done"), sem("h_done")
        h_ps, h1_done = sem("h_ps"), sem("h1_done")
        yn_done = sem("yn_done")
        pay_hi, pay_lo = sem("pay_hi"), sem("pay_lo")
        yT_ps, yT_done = sem("yT_ps"), sem("yT_done")
        logit_ps = sem("logit_ps")
        r_dve, r_exp, r_rank = sem("r_dve"), sem("r_exp"), sem("r_rank")
        ids_done = sem("ids_done")
        sent_done = [sem(f"sent_done{i}") for i in range(NY)]
        ex_in = [sem(f"ex_in{i}") for i in range(4)]
        ex_hi_done, ex_lo_done = sem("ex_hi_done"), sem("ex_lo_done")
        plan, plan_diagonals = sem("plan"), sem("plan_diagonals")
        plan_ps, plan_done = sem("plan_ps"), sem("plan_done")
        pad_rows = sem("pad_rows")
        pads_sp, pads_act = sem("pads_sp"), sem("pads_act")
        xt_in = [sem(f"xt_in{i}") for i in range(4)]
        b2_in = [sem(f"b2_in{i}") for i in range(4)]
        in_ps, in_done = sem("in_ps"), sem("in_done")
        up_ps, gelu_done, hhi_done, hlo_done = sem("up_ps"), sem("gelu_done"), sem("hhi_done"), sem("hlo_done")
        down_ps, y_done = sem("down_ps"), sem("y_done")
        tagged, dst_a, dst_b = sem("tagged"), sem("dst_a"), sem("dst_b")
        y_out = [sem(f"y_out{i}") for i in range(4)]
        bk_in = [sem(f"bk_in{i}") for i in range(NX)]
        add_a, add_b = sem("add_a"), sem("add_b")
        out_done = sem("out_done")

        N_CONST = 9
        R_EXP, R_MASK, R = 3, 18, 25
        LAST_SLOT = T - 1 + 6

        def slots(eng, step, width, first, start, high, last):
            bodies = (high + 1 - start) // width
            for n in range(first, start):
                step(At(None, n, width))
            with eng.Fori(0, bodies) as i:
                for n in range(start, start + width):
                    step(At(i, n, width))
            for n in range(start + bodies * width, last + 1):
                step(At(None, n, width))

        def slots_a(eng, step, start, high, last=LAST_SLOT):
            slots(eng, step, U, -5, start, high, last)

        def slots_b(eng, step, start, high):
            slots(eng, step, UB, -3, start, high, TILES_B + 2)

        def group_at(n):
            if n.reg is None and n.at == 3:
                return At(None, 0, 1), At(None, 0, U), 1
            if n.at % UG == 3 and n.at >= 7:
                return At(n.reg, n.at // UG, U // UG), n - (UG + 2), UG
            return None

        def place(t):
            if t.reg is None and t.at == 0:
                return At(None, 0, 1), 0
            return At(t.reg, (t.at - 1) // UG + 1, U // UG), (t.at - 1) % UG

        def through(eng, s, t):
            eng.wait_ge(s, (t + 1).val())

        def norms(n):
            there = [k for k, t in ((0, n + 2), (1, n - 1)) if t.within(0, T - 1)]
            return slice(there[0], there[-1] + 1) if there else None

        def normed(n):
            return (n + 3).val()

        def wait_alone(eng, s, v):
            v = v if isinstance(v, int) else eng.snap(v)
            eng.wait_ge(const_in, 16 * N_CONST)
            eng.wait_ge(s, v)

        def rows_of(region, row):
            return region[bass.ds(row, ROWS), :].rearrange("(p a) w -> p a w", a=HALVES)

        def rows_sent(eng, t):
            eng.wait_ge(sent_done[t.mod(NY)], (t.div(NY) + 1) * 32)

        def patches_in(eng, t):
            eng.wait_ge(x_in[(t - 1).mod(NX)], ((t - 1).div(NX) + 1) * 32)

        block = ctx.enter_context(nc.Block())

        @block.sync
        def _(sp):
            def load_patches(t):
                q = (t - 1).mod(NX)
                row = (t - 1).val() * IN_D
                sp.dma_start(xraw[q][:, 0:KC, :],
                             x[bass.ds(row, KC * P), :].rearrange("(p c) b -> p c b", c=KC)
                             ).then_inc(x_in[q], 16)
                sp.dma_start(xraw[q][0:KREST, KC, :], x[bass.ds(row + KC * P, KREST), :]
                             ).then_inc(x_in[q], 16)

            sp.wait_ge(ones_in, NX)
            load_patches(At(None, 1, U))
            for dst, src in ((cst[:, :], const),
                             (wih[:, :, :], w_ih), (whh[:, :, :], w_hh), (lbias[:, 0, :], b_ih),
                             (lbias[:, 1, :], b_hh), (rws[:, :], rw),
                             (rbs[:, :, :], rb.partition_broadcast(P)), (h0[:, 3, :], cls.partition_broadcast(P)),
                             (b1s[:, :], b1)):
                sp.dma_start(dst, src).then_inc(const_in, 16)

            def step(n):
                t = n + 6
                if t.within(2, T - 1):
                    if t.reg is not None or t.at > NX:
                        sp.wait_ge(tok_done, (t - NX).val())
                        sp.wait_ge(lo_done, (t - NX).val())
                    load_patches(t)
                t = n + 4
                if t.within(0, T - 1):
                    if t.reg is not None or t.at >= NPOS:
                        through(sp, h0_done, t - NPOS)
                    sp.dma_start(posr[:, t.mod(NPOS), :],
                                 pos[bass.ds(t.val(), 1), :].rearrange("a h -> (a h)").partition_broadcast(P)
                                 ).then_inc(pos_in[t.mod(NPOS)], 16)
                if n.within(0, PIECES - 1):
                    if n.reg is not None or n.at >= 4:
                        through(sp, ex_lo_done, n - 4)
                    sp.dma_start(ex_raw[:, n.mod(4), :], we[:, bass.ds(n.val() * PIECE, PIECE)]
                                 ).then_inc(ex_in[n.mod(4)], 16)

            slots_a(sp, step, 4, T - 7)

            sp.wait_ge(pad_rows, 1)
            for e in range(0, E, 2):
                row = sp.value_load(padi[0:1, e:e + 1], min_val=0, max_val=E * CAP - ROWS)
                sp.dma_start(rows_of(sent, row), pad[:, :, :]).then_inc(pads_sp, 16)
            for t in range(T - NY, T):
                rows_sent(sp, At(None, t, U))
            sp.wait_ge(pads_sp, 16 * E // 2)
            sp.wait_ge(pads_act, 16 * (E // 2 + 1))
            sp.wait_ge(plan_done, 1)

            def step_b(n):
                j = n + 3
                if j.within(0, TILES_B - 1):
                    if j.reg is not None or j.at >= 4:
                        through(sp, in_ps, j - 4)
                        through(sp, dst_b, j - 4)
                    row = sp.value_load(tabi[0:1, 1, bass.ds(j.val(), 1)], min_val=0, max_val=E * CAP)
                    sp.dma_start(xt[j.mod(4)], rows_of(sent, row)).then_inc(xt_in[j.mod(4)], 16)
                j = n + 1
                if j.within(0, TILES_B - 1):
                    if j.reg is not None or j.at >= 4:
                        through(sp, y_done, j - 4)
                    e = sp.value_load(tabi[0:1, 0, bass.ds(j.val(), 1)], min_val=0, max_val=E - 1)
                    sp.dma_start(b2r[:, j.mod(4), :],
                                 b2[bass.ds(e, 1), :].rearrange("a h -> (a h)").partition_broadcast(P)
                                 ).then_inc(b2_in[j.mod(4)], 16)

            slots_b(sp, step_b, 3, TILES_B - 4)

            for q in range(4):
                sp.wait_ge(y_out[q], 16 * HALVES * len(range(q, TILES_B, 4)))
            steps = T // CT

            def load(m):
                q = m % NX
                if m >= NX:
                    sp.wait_ge(add_b, (m - NX + 1) * CT)
                for k in range(2):
                    sp.dma_start(bk[q][:, k * CT:(k + 1) * CT, :],
                                 back[k * TOKENS:(k + 1) * TOKENS, :].rearrange("(b t) h -> b t h", t=T)
                                 [:, m * CT:(m + 1) * CT, :]).then_inc(bk_in[q], 16)

            for m in range(NX):
                load(m)
            for m in range(steps):
                sp.wait_ge(add_b, (m + 1) * CT)
                sp.dma_start(out[:, m * CT:(m + 1) * CT, :], h1[:, m * CT:(m + 1) * CT, :]).then_inc(out_done, 16)
                if m + NX < steps:
                    load(m + NX)
            sp.wait_ge(out_done, 16 * steps)

        @block.scalar
        def _(act):
            act.dma_start(ws[:, 0:KC, :], w).then_inc(w_in, 16)
            act.dma_start(ws[0:KBIAS + 1, KC, :], w_rest).then_inc(w_in, 16)
            act.wait_ge(setup_dve, 1)
            act.activation(tc[:, 0:1], c2[:, 0:1], ACT.Tanh)
            act.wait_ge(w_in, 32)
            act.activation(ws[:, KS:KC, :], ws[:, KS:KC, :], ACT.Copy, scale=W_SCALE)
            act.activation(ws[0:KBIAS + 1, KC, :], ws[0:KBIAS + 1, KC, :], ACT.Copy,
                           scale=W_SCALE).then_inc(setup_act, 1)
            act.activation(whi[:, :, :], ws[:, 0:KS, :], ACT.Copy, scale=W_SCALE).then_inc(setup_act, 1)
            act.wait_ge(const_in, 16 * N_CONST)
            act.activation(whh[:, :, :], whh[:, :, :], ACT.Copy, scale=0.5 * G_SCALE)
            act.activation(wih_hi[:, :, :], wih[:, :, :], ACT.Copy, scale=G_SCALE)
            act.activation(ident16[:, :], cst[:, C_ID:C_TRI], ACT.Copy)
            act.activation(tri16[:, :], cst[:, C_TRI:C_ONE], ACT.Copy)
            act.activation(ones16[:, :], cst[:, C_ONE:C_IOTA], ACT.Copy).then_inc(setup_act, 1)
            act.wait_ge(setup_dve, 4)

            def step(n):
                if n.within(0, T - 1):
                    through(act, gates_ps, n)
                    for g in range(4):
                        last = act.activation(gate[:, g, :], ps_gate[n.mod(2)][:, g * B:(g + 1) * B], ACT.Tanh,
                                              bias=lbias[:, 2, g:g + 1],
                                              scale=(1.0 if g == 2 else 0.5) / G_SCALE)
                    last.then_inc(gates_done, 1)
                t = n - 2
                if t.within(0, T - 1):
                    through(act, yT_ps, t)
                    if t.reg is not None or t.at >= 2:
                        through(act, logit_ps, t - 2)
                    act.activation(ynT[:, t.mod(2), :], ps_T[:, P:2 * P], ACT.Copy).then_inc(yT_done, 1)
                t = n + 4
                split = t.within(1, T - 1)
                if split:
                    q, r = (t - 1).mod(NX), (t - 1).mod(2)
                    patches_in(act, t)
                    if t.reg is not None or t.at > 2:
                        act.wait_ge(tok_done, (t - 2).val())
                    act.activation(xhi[r][:, 0:KS // 2, :], xraw[q][:, 0:KS // 2, :], ACT.Copy)
                if n.within(0, T - 1):
                    through(act, c_done, n)
                    act.activation(tc[:, :], c2[:, :], ACT.Tanh, scale=0.5).then_inc(tc_done, 1)
                at = group_at(n)
                if at:
                    g, t0, m = at
                    act.wait_ge(r_dve, g.val() * R + R_EXP)
                    act.activation(pr[:, 0:m, :], lg[:, 0:m, :], ACT.Exp).then_inc(r_exp, 1)
                if split:
                    act.activation(xhi[r][:, KS // 2:KS, :], xraw[q][:, KS // 2:KS, :], ACT.Copy).then_inc(hi_done, 1)
                t = n + 2
                if t.within(0, T - 1):
                    through(act, xT_ps, t)
                    if t.reg is not None or t.at >= 2:
                        through(act, gates_ps, t - 2)
                    act.activation(xT_hi[:, t.mod(2), :], ps_T[:, 0:P], ACT.Copy).then_inc(xT_hi_done, 1)
                t = n - PACK
                if t.within(0, T - 1):
                    if t.reg is not None or t.at >= NY:
                        rows_sent(act, t - NY)
                    through(act, yn_done, t)
                    act.activation(pay[:, t.mod(NY), 0:HID].bitcast(F16)[:, 0:HID], yn[:, t.mod(NY), :],
                                   ACT.Copy).then_inc(pay_hi, 1)
                if n.within(0, PIECES - 1):
                    act.wait_ge(ex_in[n.mod(4)], (n.div(4) + 1) * 16)
                    piece = ex_raw[:, n.mod(4), :]
                    flat_hi = ex_hi[:, :, :, :].rearrange("p e m f -> p (e m f)")
                    act.activation(flat_hi[:, bass.ds(n.val() * PIECE, PIECE)], piece, ACT.Copy, scale=E_SCALE)
                    act.activation(piece, piece, ACT.Copy, scale=E_SCALE).then_inc(ex_hi_done, 1)

            slots_a(act, step, U + PACK, T - 5, T - 1 + PACK)

            act.activation(tc[:, 0:1], tc[:, 0:1], ACT.Gelu)
            act.wait_ge(pad_rows, 1)
            act.dma_start(rows_of(sent, E * CAP), pad[:, :, :]).then_inc(pads_act, 16)
            for e in range(1, E, 2):
                row = act.value_load(padi[0:1, e:e + 1], min_val=0, max_val=E * CAP - ROWS)
                act.dma_start(rows_of(sent, row), pad[:, :, :]).then_inc(pads_act, 16)

            act.wait_ge(plan_done, 1)

            def step_b(n):
                j = n + 1
                if j.within(0, TILES_B - 1):
                    through(act, in_ps, j)
                    if j.reg is not None or j.at >= 2:
                        through(act, up_ps, j - 2)
                    act.activation(xTs[j.mod(2)], ps_in[j.mod(2)], ACT.Copy).then_inc(in_done, 1)
                if n.within(0, TILES_B - 1):
                    e = act.value_load(tabi[0:1, 0, bass.ds(n.val(), 1)], min_val=0, max_val=E - 1)
                    through(act, up_ps, n)
                    if n.reg is not None or n.at >= 2:
                        through(act, hlo_done, n - 2)
                    for c in range(FC):
                        last = act.activation(hf[n.mod(2)][:, c * ROWS:(c + 1) * ROWS], ps_up(n, c), ACT.Gelu,
                                              bias=b1s[:, bass.ds(e * FC + c, 1)], scale=1.0 / E_SCALE)
                    last.then_inc(gelu_done, 1)

            slots_b(act, step_b, 2, TILES_B - 2)

        @block.vector
        def _(dve):
            for q in range(NX):
                dve.memset(xraw[q][KBIAS // 2:KBIAS, KC, :], 0.0)
                dve.memset(xraw[q][KBIAS:KBIAS + 1, KC, :], 1.0).then_inc(ones_in, 1)
            dve.memset(c2[:, :], 0.0)
            dve.memset(slot[:, :, :], 0)
            dve.memset(h2[:, 1, :], 0.0)
            dve.memset(pad[:, :, :], 0.0).then_inc(setup_dve, 1)
            dve.wait_ge(setup_dve, 1)
            dve.memset(pad[:, :, HID:HID + 1].bitcast(I32), NO_TOKEN)
            dve.wait_ge(setup_act, 2)
            dve.scalar_tensor_tensor(wlo[:, :, :].rearrange("p a b -> p (a b)"),
                                     ws[:, 0:KS, :].rearrange("p a b -> p (a b)"), W_SCALE,
                                     whi[:, :, :].rearrange("p a b -> p (a b)"), ALU.mult,
                                     ALU.subtract).then_inc(setup_dve, 1)
            dve.wait_ge(const_in, 16 * N_CONST)
            dve.tensor_copy(count[:, :], cst[:, C_EBASE:C_TOK])
            dve.tensor_copy(tag[:, :, 0].bitcast(I32), cst[:, C_TOK:C_BSC])
            dve.tensor_tensor(lbias[:, 2, :], lbias[:, 0, :], lbias[:, 1, :], ALU.add).then_inc(setup_dve, 1)
            dve.wait_ge(setup_dve, 3)
            dve.tensor_tensor(lbias[:, 2, :], lbias[:, 2, :], cst[:, C_BSC:C_POW], ALU.mult).then_inc(setup_dve, 1)
            dve.wait_ge(setup_act, 3)
            dve.scalar_tensor_tensor(wih_lo[:, :, :].rearrange("p a b -> p (a b)"),
                                     wih[:, :, :].rearrange("p a b -> p (a b)"), G_SCALE,
                                     wih_hi[:, :, :].rearrange("p a b -> p (a b)"), ALU.mult,
                                     ALU.subtract).then_inc(setup_dve, 1)

            def scaled(k, src, dst, s_out):
                dve.tensor_scalar(dst, src, mv[:, k, 0:1], rstd[:, k:k + 1], ALU.subtract,
                                  ALU.mult).then_inc(s_out, 1)

            def step(n):
                t = n + 1
                if t.within(0, T - 1):
                    through(dve, xT_hi_done, t)
                    dve.tensor_tensor(xT_lo[:, t.mod(2), :], ps_T[:, 0:P], xT_hi[:, t.mod(2), :],
                                      ALU.subtract).then_inc(xT_lo_done, 1)
                if group_at(n):
                    route_logits(*group_at(n))
                t0, t1 = n + 2, n - 1
                pre, post = t0.within(0, T - 1), t1.within(0, T - 1)
                if pre:
                    src0 = h0[:, t0.mod(4), :]
                    dve.wait_ge(pos_in[t0.mod(NPOS)], (t0.div(NPOS) + 1) * 16)
                    if t0.reg is None and t0.at == 0:
                        dve.tensor_tensor(src0, h0[:, 3, :], posr[:, 0, :], ALU.mult).then_inc(h0_done, 1)
                    else:
                        dve.wait_ge(tok_done, t0.val())
                        dve.scalar_tensor_tensor(src0, ps_tok[t0.mod(2)][:, 0:HID], 1.0 / W_SCALE,
                                                 posr[:, t0.mod(NPOS), :], ALU.mult, ALU.mult).then_inc(h0_done, 1)
                if post:
                    through(dve, h_ps, t1)
                    src1 = h1[:, bass.ds(t1.val(), 1), :].rearrange("p a h -> p (a h)")
                    dve.scalar_tensor_tensor(src1, ps_h[:, 0:P], 0.5, h0[:, t1.mod(4), :], ALU.mult,
                                             ALU.add).then_inc(h1_done, 1)
                if pre:
                    wait_alone(dve, h0_done, (t0 + 1).val())
                    dve.bn_stats(stats[:, 0, :], src0).then_inc(st1, 1)
                if post:
                    wait_alone(dve, h1_done, (t1 + 1).val())
                    dve.bn_stats(stats[:, 1, :], src1).then_inc(st2, 1)
                if pre:
                    wait_alone(dve, st1, (t0 + 1).val())
                    ins = dve.bn_aggr(mv[:, 0, :], stats[:, 0, :])
                if post:
                    wait_alone(dve, st2, (t1 + 1).val())
                    ins = dve.bn_aggr(mv[:, 1, :], stats[:, 1, :])
                both = norms(n)
                if both:
                    ins.then_inc(moments, 1)
                    dve.wait_ge(moments, normed(n))
                    dve.tensor_scalar(veps[:, both], mv[:, both, 1], EPS, None, ALU.add).then_inc(veps_done, 1)
                if n.within(0, T - 1):
                    through(dve, gates_done, n)
                    dve.scalar_tensor_tensor(ca[:, :], gate[:, 1, :], 1.0, c2[:, :], ALU.add,
                                             ALU.mult).then_inc(ca_done, 1)
                    dve.scalar_tensor_tensor(cb[:, :], gate[:, 0, :], 1.0, gate[:, 2, :], ALU.add,
                                             ALU.mult).then_inc(cb_done, 1)
                    through(dve, cb_done, n)
                    through(dve, ca_done, n)
                    dve.scalar_tensor_tensor(c2[:, :], ca[:, :], 0.5, cb[:, :], ALU.mult, ALU.add).then_inc(c_done, 1)
                for k, route in enumerate((route_largest, route_first, route_second)):
                    if group_at(n - k):
                        route(*group_at(n - k))
                if both:
                    dve.wait_ge(rstd_done, normed(n))
                if pre:
                    if t0.reg is not None or t0.at >= 2:
                        through(dve, xT_ps, t0 - 2)
                    scaled(0, src0, xn[:, t0.mod(2), :], xn_done)
                if post:
                    if t1.reg is not None or t1.at >= NY:
                        through(dve, pay_lo, t1 - NY)
                        through(dve, yT_ps, t1 - NY)
                    scaled(1, src1, yn[:, t1.mod(NY), :], yn_done)
                if n.within(0, T - 1):
                    through(dve, tc_done, n)
                    dve.scalar_tensor_tensor(h2[:, n.mod(2), :], gate[:, 3, :], 1.0, tc[:, :], ALU.add,
                                             ALU.mult).then_inc(h_done, 1)
                t = n + 4
                if t.within(1, T - 1):
                    q, r = (t - 1).mod(NX), (t - 1).mod(2)
                    dve.wait_ge(hi_done, t.val())
                    dve.tensor_tensor(xlo[r][:, :, :], xraw[q][:, 0:KS, :], xhi[r][:, :, :],
                                      ALU.subtract).then_inc(lo_done, 1)
                for k, route in enumerate((route_softmax, route_first_mask, route_second_mask, route_slots)):
                    if group_at(n - k):
                        route(*group_at(n - k))

            class Group:
                def __init__(self, g, t0, m, count):
                    self.g, self.m, self.count = g, m, count
                    self.L, self.Q, self.Q2, self.K, self.iota = (
                        a[:, 0:m, :] for a in (lg, pr, pr2, cand, cst[:, C_IOTA:C_EBASE].rearrange(
                            "p (t e) -> p t e", e=E)))
                    self.OH = [oh[:, k, 0:m, :] for k in range(2)]
                    self.most = [gates[:, k, bass.ds(t0.val(), m)] for k in range(2)]
                    self.which = (tag[:, bass.ds(t0.val(), m), 1], red[:, 3, 0:m])

                def by(self, ins):
                    ins.then_inc(r_dve, 1)
                    self.count += 1

                def seen(self):
                    dve.wait_ge(r_dve, self.g.val() * R + self.count)

                def wide(self, row):
                    return row.unsqueeze(2).to_broadcast([P, self.m, E])

                def find(self, k, q):
                    self.by(dve.tensor_reduce(self.most[k], q, AX.X, ALU.max))
                    self.seen()
                    self.by(dve.tensor_tensor(self.L, q, self.wide(self.most[k]), ALU.is_lt))
                    self.seen()
                    self.by(dve.scalar_tensor_tensor(lines(self.K), lines(self.L), float(E), lines(self.iota),
                                                     ALU.mult, ALU.add))

                def mask(self, k):
                    self.by(dve.tensor_reduce(self.which[k], self.K, AX.X, ALU.min))
                    self.seen()
                    self.by(dve.tensor_tensor(self.OH[k], self.iota, self.wide(self.which[k]), ALU.is_equal))
                    self.seen()

            def lines(a):
                return a.rearrange("p t e -> p (t e)")

            def route_logits(g, t0, m):
                dve.wait_ge(logit_ps, (t0 + m).val())
                if g.reg is not None or g.at >= 1:
                    dve.wait_ge(r_dve, g.val() * R)
                dve.tensor_tensor(lg[:, 0:m, :], ps_logit[:, 0:m * E].rearrange("p (t e) -> p t e", e=E),
                                  rbs[:, 0:m, :], ALU.add).then_inc(r_dve, 1)

            def route_largest(g, t0, m):
                r = Group(g, t0, m, 1)
                r.seen()
                r.by(dve.tensor_reduce(red[:, 0, 0:m], r.L, AX.X, ALU.max))
                r.seen()
                r.by(dve.tensor_tensor(r.L, r.L, r.wide(red[:, 0, 0:m]), ALU.subtract))
                assert r.count == R_EXP

            def route_softmax(g, t0, m):
                r = Group(g, t0, m, R_EXP)
                dve.wait_ge(r_exp, (g + 1).val())
                r.by(dve.tensor_reduce(red[:, 1, 0:m], r.Q, AX.X, ALU.add))
                r.seen()
                r.by(dve.reciprocal(red[:, 2, 0:m], red[:, 1, 0:m]))
                r.seen()
                r.by(dve.tensor_tensor(r.Q, r.Q, r.wide(red[:, 2, 0:m]), ALU.mult))

            def route_first(g, t0, m):
                r = Group(g, t0, m, R_EXP + 3)
                r.seen()
                r.find(0, r.Q)

            def route_first_mask(g, t0, m):
                r = Group(g, t0, m, R_EXP + 6)
                r.seen()
                r.mask(0)
                r.by(dve.scalar_tensor_tensor(lines(r.Q2), lines(r.OH[0]), -2.0, lines(r.Q), ALU.mult, ALU.add))

            def route_second(g, t0, m):
                r = Group(g, t0, m, R_EXP + 9)
                r.seen()
                r.find(1, r.Q2)

            def route_second_mask(g, t0, m):
                r = Group(g, t0, m, R_EXP + 12)
                r.seen()
                r.mask(1)
                r.by(dve.tensor_tensor(mask16[:, 0:m, :], r.OH[0], r.OH[1], ALU.add))
                assert r.count == R_MASK

            def route_slots(g, t0, m):
                r = Group(g, t0, m, R_MASK)
                dve.wait_ge(r_rank, (g + 1).val())
                r.by(dve.tensor_tensor(rank[:, 0:m, :], ps_rank[:, 0:m * E].rearrange("p (t e) -> p t e", e=E),
                                       count[:, :].unsqueeze(1).to_broadcast([P, m, E]), ALU.add))
                r.seen()
                r.by(dve.tensor_tensor(count[:, :], count[:, :], ps_rank[:, m * E:(m + 1) * E], ALU.add))
                r.by(dve.tensor_tensor(r.K, rank[:, 0:m, :], r.OH[0], ALU.mult))
                r.by(dve.tensor_tensor(r.Q2, rank[:, 0:m, :], r.OH[1], ALU.mult))
                r.seen()
                r.by(dve.tensor_reduce(slotf[:, 0, 0:m], r.K, AX.X, ALU.add))
                r.by(dve.tensor_reduce(slotf[:, 1, 0:m], r.Q2, AX.X, ALU.add))
                r.seen()
                if g.reg is not None or g.at >= 1:
                    dve.wait_ge(ids_done, g.val())
                r.by(dve.tensor_copy(slot[:, :, 0:m], slotf[:, :, 0:m]))
                assert r.count == R

            slots_a(dve, step, 1 + NY, T - 5)

            done = [0]

            def by(ins):
                ins.then_inc(plan, 1)
                done[0] += 1

            def seen():
                dve.wait_ge(plan, done[0])

            dve.wait_ge(r_dve, R * GROUPS)
            dve.tensor_copy(padi[:, :], count[0:1, :]).then_inc(pad_rows, 1)
            by(dve.tensor_tensor(tabs[:, 0, :], count[:, :], cst[:, C_EBASE:C_TOK], ALU.subtract))
            seen()
            whole = [tabs[:, k, :].bitcast(I32) for k in (1, 2)]
            shift = ROWS.bit_length() - 1
            by(dve.tensor_scalar(whole[0], tabs[:, 0, :], float(ROWS - 1), None, ALU.add))
            seen()
            by(dve.tensor_scalar(whole[1], whole[0], shift, shift, ALU.logical_shift_right, ALU.logical_shift_left))
            seen()
            by(dve.tensor_copy(tabs[:, 3, :], whole[1]))
            seen()
            length, row = tabs[:, 3, :], 3
            for k in (1, 2, 4, 8):
                by(dve.tensor_tensor(tabs[:, row + 1, k:E], tabs[:, row, k:E], tabs[:, row, 0:E - k], ALU.add))
                by(dve.tensor_copy(tabs[:, row + 1, 0:k], tabs[:, row, 0:k]))
                seen()
                row += 1
            ends, over, over_length = tabs[:, row, :], tabs[:, row + 1, :], tabs[:, row + 2, :]
            start, expert, before = cst[:, C_J:C_END], tab1[:, 0:1], tab1[:, 1:2]
            by(dve.tensor_scalar(over, ends, start, None, ALU.is_le))
            seen()
            by(dve.tensor_tensor(over_length, over, length, ALU.mult))
            by(dve.tensor_reduce(expert, over, AX.X, ALU.add))
            seen()
            by(dve.tensor_reduce(before, over_length, AX.X, ALU.add))
            seen()
            by(dve.tensor_tensor(tab1[:, 2:3], start, before, ALU.subtract))
            seen()
            for k, column in enumerate((expert, tab1[:, 2:3])):
                dve.tensor_scalar(diagonals[:, k, :], cst[:, C_ID:C_ID + TILES_B], column, None,
                                  ALU.mult).then_inc(plan_diagonals, 1)
            dve.wait_ge(plan_ps, 1)
            by(dve.tensor_copy(tabj[:, :, :].rearrange("p a j -> p (a j)"), ps_rank[:, 0:2 * TILES_B]))
            seen()
            by(dve.tensor_scalar(tabi[:, 0, :], tabj[0:1, 0, :], float(E - 1), None, ALU.min))
            by(dve.scalar_tensor_tensor(tabj[0:1, 1, :], tabj[0:1, 0, :], float(CAP), tabj[0:1, 1, :], ALU.mult,
                                        ALU.add))
            seen()
            dve.tensor_scalar(tabi[:, 1, :], tabj[0:1, 1, :], float(E * CAP), None, ALU.min).then_inc(plan_done, 1)
            dve.tensor_scalar(tabj[:, 0, :], tabj[:, 0, :], float(E - 1), None, ALU.min).then_inc(plan_done, 1)
            dve.wait_ge(plan_done, 2)

            def step_b(n):
                if n.within(0, TILES_B - 1):
                    q = n.mod(4)
                    dve.wait_ge(xt_in[q], (n.div(4) + 1) * 16)
                    if n.reg is not None or n.at >= 4:
                        dve.wait_ge(y_out[q], n.div(4) * 16 * HALVES)
                    dve.tensor_scalar(dsto[q], xt[q][:, :, HID + 1], tabj[:, 0, bass.ds(n.val(), 1)],
                                      float(TOKENS), ALU.not_equal, ALU.mult).then_inc(dst_a, 1)
                j = n - 2
                if j.within(0, TILES_B - 1):
                    q = j.mod(4)
                    through(dve, down_ps, j)
                    dve.wait_ge(b2_in[q], (j.div(4) + 1) * 16)
                    dve.scalar_tensor_tensor(yo[q], ps_down[j.mod(2)][:, 0:HALVES * HID].rearrange(
                                                 "p (a h) -> p a h", a=HALVES), 1.0 / E_SCALE,
                                             b2r[:, q, :].unsqueeze(1).to_broadcast([P, HALVES, HID]), ALU.mult,
                                             ALU.add).then_inc(y_done, 1)
                if n.within(0, TILES_B - 1):
                    through(dve, gelu_done, n)
                    if n.reg is not None or n.at >= 4:
                        through(dve, down_ps, n - 4)
                    dve.tensor_copy(hhi[n.mod(4)], hf[n.mod(2)]).then_inc(hhi_done, 1)
                    through(dve, hhi_done, n)
                    dve.tensor_tensor(hlo[n.mod(4)], hf[n.mod(2)], hhi[n.mod(4)], ALU.subtract).then_inc(hlo_done, 1)

            slots_b(dve, step_b, 6, TILES_B - 1)

            for m in range(T // CT):
                q = m % NX
                dve.wait_ge(bk_in[q], 32 * (m // NX + 1))
                for k, s in ((0, add_a), (1, add_b)):
                    for i in range(CT):
                        t = m * CT + i
                        if k == 1:
                            dve.wait_ge(add_a, t + 1)
                        dve.scalar_tensor_tensor(h1[:, t, :], bk[q][:, k * CT + i, :], gates[:, k, t:t + 1],
                                                 h1[:, t, :], ALU.mult, ALU.add).then_inc(s, 1)

        @block.gpsimd
        def _(pool):
            pool.wait_ge(const_in, 16 * N_CONST)

            def sends_in(n):
                t = n - SEND
                if n.reg is None and n.at >= T - 2:
                    r = (t.at - 1) % UG
                    return [t + r, t + (r + 1)] if 2 * r < UG and (t + r).within(0, T - 1) else []
                return [t] if t.within(0, T - 1) else []

            def step(n):
                sends = [(t, *place(t)) for t in sends_in(n)]
                for t, g, col in sends:
                    if col == 0:
                        pool.wait_ge(r_dve, (g.val() + 1) * R)
                        for k in range(UG + 1, 2 * UG + 1):
                            if t.reg is not None or t.at >= k:
                                rows_sent(pool, t - k)
                both = norms(n)
                if both:
                    pool.wait_ge(veps_done, normed(n))
                    pool.tensor_tensor(rstd[:, both], veps[:, both],
                                       cst[:, C_POW:C_POW + 1].to_broadcast([P, both.stop - both.start]),
                                       ALU.pow).then_inc(rstd_done, 1)
                for t, g, col in sends:
                    if col == 0:
                        pool.tensor_copy(slot_own[:, g.mod(2), :, :], slot[:, :, :]).then_inc(ids_done, 1)
                    pool.tensor_copy(pay[:, t.mod(NY), HID:ROW].bitcast(I32),
                                     tag[:, bass.ds(t.val(), 1), :].rearrange("p a w -> p (a w)").bitcast(I32)
                                     ).then_inc(tagged, 1)
                for t, g, col in sends[-1:]:
                    pool.wait_ge(ids_done, (g + 1).val())
                    through(pool, tagged, t)
                    through(pool, pay_lo, t)
                piece = n - 1
                if piece.within(0, PIECES - 1):
                    through(pool, ex_hi_done, piece)
                    flat_hi = ex_hi[:, :, :, :].rearrange("p e m f -> p (e m f)")
                    flat_lo = ex_lo[:, :, :, :].rearrange("p e m f -> p (e m f)")
                    here = bass.ds(piece.val() * PIECE, PIECE)
                    pool.tensor_tensor(flat_lo[:, here], ex_raw[:, piece.mod(4), :], flat_hi[:, here],
                                       ALU.subtract).then_inc(ex_lo_done, 1)
                for t, g, col in sends:
                    for k in range(2):
                        pool.indirect_dma_start(
                            sent, bass.IndirectOffsetOnAxis(ap=slot_own[:, g.mod(2), k, col:col + 1], axis=0),
                            pay[:, t.mod(NY), :], None, bounds_check=E * CAP - 1, oob_is_err=False
                        ).then_inc(sent_done[t.mod(NY)], 16)
                t = n - PACK
                if t.within(0, T - 1):
                    halves = pay[:, t.mod(NY), 0:HID].bitcast(F16)
                    through(pool, pay_hi, t)
                    pool.tensor_tensor(halves[:, HID:2 * HID], yn[:, t.mod(NY), :], halves[:, 0:HID],
                                       ALU.subtract).then_inc(pay_lo, 1)

            slots_a(pool, step, SEND + 2 * UG + 1, PIECES - 1, T - 1 + SEND)

            def step_b(n):
                j = n - 2
                sends = j.within(0, TILES_B - 1)
                if sends:
                    through(pool, dst_b, j)
                    through(pool, y_done, j)
                if n.within(0, TILES_B - 1):
                    through(pool, dst_a, n)
                    q = n.mod(4)
                    pool.tensor_tensor(dsti[q], dsto[q], xt[q][:, :, HID].bitcast(I32), ALU.add).then_inc(dst_b, 1)
                if sends:
                    q = j.mod(4)
                    for k in range(HALVES):
                        pool.indirect_dma_start(back, bass.IndirectOffsetOnAxis(ap=dsti[q][:, k:k + 1], axis=0),
                                                yo[q][:, k, :], None, bounds_check=2 * TOKENS - 1,
                                                oob_is_err=False).then_inc(y_out[q], 16)

            pool.wait_ge(plan_done, 1)
            slots_b(pool, step_b, 6, TILES_B - 1)

        @block.tensor
        def _(pe):
            pe.wait_ge(setup_act, 1)
            ident = cst[:, C_ID:C_TRI]

            def project(t, a, b):
                bank_of, q, r = ps_tok[t.mod(2)][:, 0:HID], (t - 1).mod(NX), (t - 1).mod(2)
                for c in range(a, b):
                    if c < KS:
                        parts = [(l[r][:, c, :], w_[:, c, :]) for l, w_ in ((xhi, whi), (xhi, wlo), (xlo, whi))]
                    else:
                        rows = slice(0, P if c < KC else KBIAS + 1)
                        parts = [(xraw[q][rows, c, :], ws[rows, c, :])]
                    for k, (l, w_) in enumerate(parts):
                        last = pe.matmul(bank_of, l, w_, start=(c == KS and k == 0), stop=(c == KS - 1 and k == 2))
                return last

            def step(n):
                if n.within(0, T - 1):
                    if n.reg is not None or n.at >= 1:
                        through(pe, h_done, n - 1)
                    for g in range(4):
                        last = pe.matmul(ps_gate[n.mod(2)][:, g * B:(g + 1) * B], whh[:, g, :],
                                         h2[:, (n - 1).mod(2), :], start=False, stop=True, skip_group_check=True)
                    last.then_inc(gates_ps, 1)
                t = n - 1
                if t.within(0, T - 1):
                    through(pe, h_done, t)
                    if t.reg is not None or t.at >= 1:
                        through(pe, h1_done, t - 1)
                    pe.transpose(ps_h[:, 0:P], h2[:, t.mod(2), :], ident).then_inc(h_ps, 1)
                t = n - 2
                if t.within(0, T - 1):
                    through(pe, yn_done, t)
                    if (t + 3).within(0, T - 1):
                        through(pe, xT_lo_done, t + 3)
                    if t.reg is not None or t.at >= 1:
                        through(pe, yT_done, t - 1)
                    pe.transpose(ps_T[:, P:2 * P], yn[:, t.mod(NY), :], ident).then_inc(yT_ps, 1)
                t = n + 1
                if t.within(0, T - 1):
                    through(pe, xT_lo_done, t)
                    if t.reg is not None or t.at >= 2:
                        through(pe, gates_done, t - 2)
                    for g in range(4):
                        for k, (w_, r) in enumerate(((wih_hi, xT_hi), (wih_hi, xT_lo), (wih_lo, xT_hi))):
                            pe.matmul(ps_gate[t.mod(2)][:, g * B:(g + 1) * B], w_[:, g, :], r[:, t.mod(2), :],
                                      start=(g == 0 and k == 0), stop=False, skip_group_check=True)
                at = group_at(n - 3)
                if at:
                    g, t0, m = at
                    pe.wait_ge(r_dve, g.val() * R + R_MASK)
                    pe.matmul(ps_rank[:, 0:m * E], tri16[:, :], mask16[:, 0:m, :], start=True, stop=False,
                              skip_group_check=True)
                    for k in range(1, m + 1):
                        last = pe.matmul(ps_rank[:, k * E:(m + 1) * E], ones16[:, :], mask16[:, 0:m + 1 - k, :],
                                         start=False, stop=(k == m), skip_group_check=True)
                    last.then_inc(r_rank, 1)
                t = n + 3
                proj = t.within(1, T - 1)
                if proj:
                    patches_in(pe, t)
                    if t.reg is not None or t.at > 2:
                        through(pe, h0_done, t - 2)
                    project(t, KS, KC + 1)
                    if t.reg is None and t.at == 1:
                        pe.wait_ge(const_in, 16 * N_CONST)
                        pe.wait_ge(setup_act, 3)
                        pe.wait_ge(setup_dve, 5)
                if proj:
                    pe.wait_ge(lo_done, (n + 3).val())
                    project(n + 3, 0, KS).then_inc(tok_done, 1)
                t = n + 2
                if t.within(0, T - 1):
                    through(pe, xn_done, t)
                    if t.reg is not None or t.at >= 4:
                        through(pe, yT_done, t - 4)
                    pe.transpose(ps_T[:, 0:P], xn[:, t.mod(2), :], ident).then_inc(xT_ps, 1)
                t = n - 2
                if t.within(0, T - 1):
                    through(pe, yT_done, t)
                    g, col = place(t)
                    if col == 0 and t.at > 0:
                        pe.wait_ge(r_dve, (g - 1).val() * R + 1)
                    pe.matmul(ps_logit[:, col * E:(col + 1) * E], ynT[:, t.mod(2), :], rws[:, :], start=True,
                              stop=True).then_inc(logit_ps, 1)
            slots_a(pe, step, 7, T - 4)
            pe.wait_ge(plan_diagonals, 2)
            pe.matmul(ps_rank[:, 0:2 * TILES_B], cst[:, C_ONE:C_IOTA],
                      diagonals[:, :, :].rearrange("p a j -> p (a j)"), start=True, stop=True).then_inc(plan_ps, 1)
            pe.wait_ge(plan_done, 1)
            pe.wait_ge(ex_lo_done, PIECES)
            pe.wait_ge(gates_done, T)
            pe.wait_ge(yT_done, T)
            expert = [pe.alloc_register(f"expert{i}") for i in range(4)]

            def step_b(n):
                j = n + 1
                if j.within(0, TILES_B - 1):
                    pe.wait_ge(xt_in[j.mod(4)], (j.div(4) + 1) * 16)
                    for a in range(HALVES):
                        parts = xt[j.mod(4)][:, a, 0:HID].bitcast(F16)
                        for k in range(2):
                            last = pe.transpose(ps_in[j.mod(2)][:, k * ROWS + a * P:k * ROWS + (a + 1) * P],
                                                parts[:, k * P:(k + 1) * P], ident16[:, :])
                    last.then_inc(in_ps, 1)
                if n.within(0, TILES_B - 1):
                    pe.reg_load(expert[n.mod(4)], tabi[0:1, 0, bass.ds(n.val(), 1)])
                    e = pe.snap(expert[n.mod(4)], min_val=0, max_val=E - 1)
                    through(pe, in_done, n)
                    x_hi, x_lo = xTs[n.mod(2)][:, 0:ROWS], xTs[n.mod(2)][:, ROWS:2 * ROWS]
                    for c in range(FC):
                        for k, (w_, r) in enumerate(((ex_hi, x_hi), (ex_hi, x_lo), (ex_lo, x_hi))):
                            w1 = w_[:, bass.ds(e, 1), 0, c * P:(c + 1) * P].rearrange("p a f -> p (a f)")
                            last = pe.matmul(ps_up(n, c), w1, r, start=(k == 0), stop=(k == 2))
                    last.then_inc(up_ps, 1)
                j = n - 2
                if j.within(0, TILES_B - 1):
                    e = pe.snap(expert[j.mod(4)], min_val=0, max_val=E - 1)
                    through(pe, hlo_done, j)
                    for c in range(FC):
                        for k, (h_, w_) in enumerate(((hhi, ex_hi), (hlo, ex_hi), (hhi, ex_lo))):
                            w2 = w_[:, bass.ds(e, 1), 1, c * HID:(c + 1) * HID].rearrange("p a f -> p (a f)")
                            for a in range(HALVES):
                                h = h_[j.mod(4)][:, c * ROWS + a * P:c * ROWS + (a + 1) * P]
                                last = pe.matmul(ps_down[j.mod(2)][:, a * HID:(a + 1) * HID], h, w2,
                                                 start=(c == 0 and k == 0 and a == 0), stop=(c == FC - 1 and k == 2),
                                                 skip_group_check=True)
                    last.then_inc(down_ps, 1)

            slots_b(pe, step_b, 4, TILES_B - 2)


def kernel(**inputs):
    import concourse.bacc as bacc
    from concourse.bass_utils import run_bass_kernel_spmd as run

    a = {k: np.asarray(v) for k, v in inputs.items()}

    def whole(v):
        return np.ascontiguousarray(v)

    x = a["x"].reshape(B, C, GRID, PATCH, GRID, PATCH).transpose(2, 4, 1, 3, 5, 0)
    w = a["L0_tok_W"].T
    w1 = a["L0_ffn_w1"].transpose(2, 0, 1)
    w2 = a["L0_ffn_w2"].reshape(E, HID, FC, P).transpose(3, 0, 2, 1)
    arrays = {
        "x": whole(x).reshape((T - 1) * IN_D, B),
        "w": whole(w[:KC * P]).reshape(P, KC, HID),
        "w_rest": whole(np.concatenate([w[KC * P:], np.zeros((KBIAS - KREST, HID), np.float32),
                                        a["L0_tok_b"].reshape(1, HID)])),
        "cls": whole(a["L0_tok_class_token"]).reshape(HID),
        "pos": whole(a["L0_tok_pos_embed"]),
        "w_ih": whole(a["L0_attn_W_ih"].reshape(4, HID, HID).transpose(2, 0, 1)),
        "w_hh": whole(a["L0_attn_W_hh"].reshape(4, HID, HID).transpose(2, 0, 1)),
        "b_ih": whole(a["L0_attn_b_ih"].reshape(4, HID).T),
        "b_hh": whole(a["L0_attn_b_hh"].reshape(4, HID).T),
        "rw": whole(a["L0_ffn_router_w"].T),
        "rb": whole(np.broadcast_to(a["L0_ffn_router_b"], (UG, E))),
        "we": whole(np.stack([w1, w2.reshape(P, E, FC * HID)], axis=2)).reshape(P, E * 2 * FF),
        "b1": whole(a["L0_ffn_b1"].reshape(E, FC, P).transpose(2, 0, 1)).reshape(P, E * FC),
        "b2": whole(a["L0_ffn_b2"]),
        "const": constants(),
    }
    nc = bacc.Bacc("TRN2", target_bir_lowering=False, num_devices=1)
    args = {k: nc.dram_tensor(f"in_{k}", list(v.shape), mybir.dt.from_np(v.dtype), kind="ExternalInput").ap()
            for k, v in arrays.items()}
    out = nc.dram_tensor("out_tower", [B, T, HID], mybir.dt.float32, kind="ExternalOutput").ap()
    tower(nc, out=out, **args)
    r = run(nc, [{f"in_{k}": v for k, v in arrays.items()}], core_ids=[0])
    return r.results[0]["out_tower"]
```
